# Optimizing a Trainium2 kernel written in Bass

```python
import numpy as np
import jax
import jax.numpy as jnp

def _softmax(x, axis=-1):
    return jax.nn.softmax(x, axis=axis)

def _gelu(x):
    return jax.nn.gelu(x, approximate=True)

def _silu(x):
    return jax.nn.silu(x)

def _sigmoid(x):
    return jax.nn.sigmoid(x)

def _layernorm(x, axis=-1, eps=1e-05):
    m = jnp.mean(x, axis=axis, keepdims=True)
    v = jnp.var(x, axis=axis, keepdims=True)
    return (x - m) / jnp.sqrt(v + eps)

def _scatter_add(tgt, idx, src, axis=0):
    return tgt.at[idx].add(src)

def _segment_sum(src, seg, n):
    return jax.ops.segment_sum(src, seg, n)
kernel_name = 'mk_macaron_d1_jaxref_r8_eff86d'

def setup_inputs(seed: int=0):
    np.random.seed(seed)
    _w = jnp.asarray

    def _L0_attn_setup():
        import jax, jax.numpy as jnp
        import numpy as np
        _J6 = jnp.array([[0, 0, 0, 0, 0, 1], [0, 0, 0, 0, -1, 0], [0, 0, 0, 1, 0, 0], [0, 0, 1, 0, 0, 0], [0, -1, 0, 0, 0, 0], [1, 0, 0, 0, 0, 0]], dtype=jnp.float32)
        _PI = np.array([0, 0, 0, 1, 1, 2])
        _PJ = np.array([1, 2, 3, 2, 3, 3])

        def plucker_lines(p1, p2):
            lines = p1[..., _PI] * p2[..., _PJ] - p1[..., _PJ] * p2[..., _PI]
            n = jnp.linalg.norm(lines, axis=-1, keepdims=True)
            return lines / jnp.maximum(n, 1e-12)
        key = jax.random.key(seed)
        ks = jax.random.split(key, 6)
        B, T, D, H = (1, 256, 128, 16)
        s = D ** (-0.5)
        x = jax.random.normal(ks[0], (B, T, D), jnp.float32)
        Wqkv = jax.random.normal(ks[1], (D, 3 * D), jnp.float32) * s
        bqkv = jnp.zeros((3 * D,), jnp.float32)
        W1p = jax.random.normal(ks[2], (D, 4 * H), jnp.float32) * s
        W2p = jax.random.normal(ks[3], (D, 4 * H), jnp.float32) * s
        plucker_scale = jnp.full((H,), 0.1, jnp.float32)
        Wout = jax.random.normal(ks[4], (D, D), jnp.float32) * s
        bout = jnp.zeros((D,), jnp.float32)
        return {'x': x, 'Wqkv': Wqkv, 'bqkv': bqkv, 'W1p': W1p, 'W2p': W2p, 'plucker_scale': plucker_scale, 'Wout': Wout, 'bout': bout}
    _L0_attn_in = _L0_attn_setup()

    def _L0_ffn_setup():
        import jax, jax.numpy as jnp
        import numpy as np
        B, S, H = (2, 128, 128)
        E, F = (8, 512)
        GATE_TEMP = 0.1
        key = jax.random.key(seed)
        ks = jax.random.split(key, 6)
        s_h = 1.0 / np.sqrt(H)
        s_f = 1.0 / np.sqrt(F)
        return {'hidden_states': jax.random.normal(ks[0], (B, S, H), dtype=jnp.float32), 'w_router': jax.random.normal(ks[1], (H, E), dtype=jnp.float32) * s_h, 'w_gating': jax.random.normal(ks[2], (H, E), dtype=jnp.float32) * s_h, 'w_gate': jax.random.normal(ks[3], (E, H, F), dtype=jnp.float32) * s_h, 'w_up': jax.random.normal(ks[4], (E, H, F), dtype=jnp.float32) * s_h, 'w_down': jax.random.normal(ks[5], (E, F, H), dtype=jnp.float32) * s_f}
    _L0_ffn_in = _L0_ffn_setup()
    _d = {'L0_attn_x': _L0_attn_in['x'], 'L0_attn_Wqkv': _L0_attn_in['Wqkv'], 'L0_attn_bqkv': _L0_attn_in['bqkv'], 'L0_attn_W1p': _L0_attn_in['W1p'], 'L0_attn_W2p': _L0_attn_in['W2p'], 'L0_attn_plucker_scale': _L0_attn_in['plucker_scale'], 'L0_attn_Wout': _L0_attn_in['Wout'], 'L0_attn_bout': _L0_attn_in['bout'], 'L0_ffn_w_router': _L0_ffn_in['w_router'], 'L0_ffn_w_gating': _L0_ffn_in['w_gating'], 'L0_ffn_w_gate': _L0_ffn_in['w_gate'], 'L0_ffn_w_up': _L0_ffn_in['w_up'], 'L0_ffn_w_down': _L0_ffn_in['w_down']}
    _x0 = _d['L0_attn_x']
    _d['L0_attn_x'] = jax.random.normal(jax.random.fold_in(jax.random.key(seed), 1), (8, 512, 128), dtype=_x0.dtype)
    del _x0
    return _d

def reference(L0_attn_x, L0_attn_Wqkv, L0_attn_bqkv, L0_attn_W1p, L0_attn_W2p, L0_attn_plucker_scale, L0_attn_Wout, L0_attn_bout, L0_ffn_w_router, L0_ffn_w_gating, L0_ffn_w_gate, L0_ffn_w_up, L0_ffn_w_down):

    def _L0_attn_ref(x, Wqkv, bqkv, W1p, W2p, plucker_scale, Wout, bout):
        import jax, jax.numpy as jnp
        import numpy as np
        _J6 = jnp.array([[0, 0, 0, 0, 0, 1], [0, 0, 0, 0, -1, 0], [0, 0, 0, 1, 0, 0], [0, 0, 1, 0, 0, 0], [0, -1, 0, 0, 0, 0], [1, 0, 0, 0, 0, 0]], dtype=jnp.float32)
        _PI = np.array([0, 0, 0, 1, 1, 2])
        _PJ = np.array([1, 2, 3, 2, 3, 3])

        def plucker_lines(p1, p2):
            lines = p1[..., _PI] * p2[..., _PJ] - p1[..., _PJ] * p2[..., _PI]
            n = jnp.linalg.norm(lines, axis=-1, keepdims=True)
            return lines / jnp.maximum(n, 1e-12)
        B, T, D = x.shape
        H = plucker_scale.shape[0]
        dh = D // H
        qkv = (x @ Wqkv + bqkv).reshape(B, T, 3, H, dh)
        q = jnp.transpose(qkv[:, :, 0], (0, 2, 1, 3))
        k = jnp.transpose(qkv[:, :, 1], (0, 2, 1, 3))
        v = jnp.transpose(qkv[:, :, 2], (0, 2, 1, 3))
        std_logits = jnp.einsum('bhid,bhjd->bhij', q, k) * dh ** (-0.5)
        p1 = (x @ W1p).reshape(B, T, H, 4)
        p2 = (x @ W2p).reshape(B, T, H, 4)
        lines_h = jnp.transpose(plucker_lines(p1, p2), (0, 2, 1, 3))
        Jlines = lines_h @ _J6.T
        plucker_bias = jnp.einsum('bhic,bhjc->bhij', lines_h, Jlines)
        logits = std_logits + plucker_bias * plucker_scale[None, :, None, None]
        causal = jnp.triu(jnp.ones((T, T), bool), 1)
        logits = jnp.where(causal[None, None], -jnp.inf, logits)
        attn = jax.nn.softmax(logits, axis=-1)
        out = jnp.einsum('bhij,bhjd->bhid', attn, v)
        out = jnp.transpose(out, (0, 2, 1, 3)).reshape(B, T, D)
        return out @ Wout + bout

    def _L0_ffn_ref(hidden_states, w_router, w_gating, w_gate, w_up, w_down):
        import jax, jax.numpy as jnp
        import numpy as np
        B, S, H = (2, 128, 128)
        E, F = (8, 512)
        GATE_TEMP = 0.1
        x = hidden_states
        router_probs = jax.nn.softmax(jnp.einsum('bsh,he->bse', x, w_router), axis=-1)
        gate_weights = jax.nn.softmax(jnp.einsum('bsh,he->bse', x, w_gating) / GATE_TEMP, axis=-1)
        g = jnp.einsum('bsh,ehf->ebsf', x, w_gate)
        u = jnp.einsum('bsh,ehf->ebsf', x, w_up)
        h = jax.nn.silu(g) * u
        expert_out = jnp.einsum('ebsf,efh->ebsh', h, w_down)
        cw = router_probs * gate_weights
        cw = cw / (jnp.sum(cw, axis=-1, keepdims=True) + 1e-09)
        out = jnp.einsum('ebsh,bse->bsh', expert_out, cw)
        return out
    x = L0_attn_x
    x = x + 0.5 * _L0_ffn_ref(_layernorm(x, axis=-1), L0_ffn_w_router, L0_ffn_w_gating, L0_ffn_w_gate, L0_ffn_w_up, L0_ffn_w_down)
    x = x + _L0_attn_ref(_layernorm(x, axis=-1), L0_attn_Wqkv, L0_attn_bqkv, L0_attn_W1p, L0_attn_W2p, L0_attn_plucker_scale, L0_attn_Wout, L0_attn_bout)
    x = x + 0.5 * _L0_ffn_ref(_layernorm(x, axis=-1), L0_ffn_w_router, L0_ffn_w_gating, L0_ffn_w_gate, L0_ffn_w_up, L0_ffn_w_down)
    return x

_drawn_inputs = setup_inputs


def setup_inputs(seed=0):
    import zlib

    import numpy as np

    out = dict(_drawn_inputs(seed))
    spreads = {'L0_attn_bqkv': (0.0, 0.1),
     'L0_attn_plucker_scale': (0.10000000149011612, 0.2),
     'L0_attn_bout': (0.0, 0.1)}
    factors = {}
    for name, (base, spread) in spreads.items():
        noise = np.random.default_rng([zlib.crc32(name.encode()), seed]).standard_normal(out[name].shape)
        drawn = base * np.exp(spread * noise) if base else spread * noise
        out[name] = jnp.asarray(drawn.astype(out[name].dtype))
    for name, factor in factors.items():
        out[name] = (out[name] * factor).astype(out[name].dtype)
    return out
```

```python
from contextlib import ExitStack
import math

import concourse.bass as bass
from concourse import mybir

F32 = mybir.dt.float32
F32R = mybir.dt.float32r
ALU = mybir.AluOpType
ACT = mybir.ActivationFunctionType
AX_X = mybir.AxisListType.X

P = 128
BANK = 512
EPS = 1e-5
LN_SCALE = 16


class Count:

    def __init__(self):
        self.base, self.local = 0, 0

    def now(self):
        return self.base + self.local

    def step(self, k=1):
        self.local += k
        return self.now()

    def enter(self, i, per_round):
        self.outer = self.base + self.local
        self.base, self.local = self.outer + i * per_round, 0

    def leave(self, rounds, per_round):
        assert self.local == per_round, (self.local, per_round)
        self.base, self.local = self.outer + rounds * per_round, 0


def attention_phase(nc, psum, x_sb, ident, dram):
    NT, D = x_sb.shape[1:]
    H = dram["scale"].shape[0]
    DH = D // H
    NC = 6
    C = DH + NC
    K = 3 * C + 1
    HP = 64
    NP = H // 2
    IT = BANK // P
    NB = NT // IT
    VW = 32
    assert DH == 8 and NP == 8 and K <= HP and NB >= 3
    QSCALE = float(DH) ** -0.5

    with ExitStack() as ctx:
        def sb(name, shape, dt=F32):
            return ctx.enter_context(nc.sbuf_tensor("a_" + name, shape, dt))

        def sem(name):
            return ctx.enter_context(nc.semaphore("a_" + name))

        w_raw = sb("w_raw", [P, BANK])
        w_hi = sb("w_hi", [P, BANK], F32R)
        w_lo = sb("w_lo", [P, BANK], F32R)
        wo_raw = sb("wo_raw", [P, D])
        wo_hi = sb("wo_hi", [P, D], F32R)
        wo_lo = sb("wo_lo", [P, D], F32R)
        bias = sb("bias", [P, BANK])
        bout = sb("bout", [P, D])
        pscale = sb("pscale", [P, H])
        sign = sb("sign", [P, NC])
        causal = sb("causal", [P, BANK])
        stats = sb("stats", [P, NT, 6])
        mv = sb("mv", [P, NT, 2])
        var = sb("var", [P, NT])
        rstd = sb("rstd", [P, NT])
        newton = sb("newton", [P, NT])
        xn = sb("xn", [P, BANK])
        xt_hi = sb("xt_hi", [P, BANK], F32R)
        xt_lo = sb("xt_lo", [P, BANK], F32R)
        raw = sb("raw", [P, IT, BANK])
        la = sb("la", [P, IT * H, NC])
        lb = sb("lb", [P, IT * H, NC])
        ss = sb("ss", [P, IT * H])
        rn = sb("rn", [P, IT * H])
        half_ln = sb("half_ln", [P, 1])
        nw = sb("nw", [P, IT * H])
        qf = sb("qf", [P, IT * H, C])
        kf = sb("kf", [P, IT * H, C])
        qcat = sb("qcat", [P, IT * H, HP])
        kcat = sb("kcat", [P, IT * H, HP])
        qt = sb("qt", [P, NP, BANK], F32R)
        kt = sb("kt", [P, NP, BANK], F32R)
        mx = sb("mx", [P, 2, 2, 4, IT])
        mt = sb("mt", [2 * 4 * IT, 2, P], F32R)
        junk = sb("junk", [P, 2, BANK])
        gate_dve = sb("gate_dve", [P, 6 * NP])
        gate_pool = sb("gate_pool", [P, 3 * NP])
        probs = sb("probs", [P, 2, 5 * BANK])
        v_sb = sb("v_sb", [P, IT * H, VW])
        ao_t = sb("ao_t", [P, H // 4, BANK])
        rec = sb("rec", [P, 2, H])
        ao = sb("ao", [P, IT, D])
        aot_hi = sb("aot_hi", [P, BANK], F32R)
        aot_lo = sb("aot_lo", [P, BANK], F32R)

        ld = sem("ld")
        const = sem("const")
        link_dve = sem("link_dve")
        var_done = sem("var_done")
        rstd_done = sem("rstd_done")
        w_done = sem("w_done")
        xn_done = sem("xn_done")
        bout_added = sem("bout_added")
        x_added = sem("x_added")
        t_full = sem("t_full")
        t_half = sem("t_half")
        t_free = sem("t_free")
        m_full = [sem(f"m_full{i}") for i in range(2)]
        m_free = [sem(f"m_free{i}") for i in range(2)]
        s_full = sem("s_full")
        s_free = sem("s_free")
        masked = sem("masked")
        pv_done = sem("pv_done")
        pv_free = sem("pv_free")
        ss_done = sem("ss_done")
        rn_done = sem("rn_done")
        cats_done = sem("cats_done")
        v_done = sem("v_done")
        mt_done = sem("mt_done")
        m_row = [sem(f"m_row{i}") for i in range(2)]

        S = [psum[:, 0:2, :], psum[:, 2:4, :]]
        M = [psum[:, 4, :], psum[:, 5, :]]
        T = psum[:, 6, :]
        PV = psum[:, 7, :]

        def wait(eng, s, value):
            if not (isinstance(value, int) and value <= 0):
                eng.wait_ge(s, value)

        def pipeline(eng, body, counts):
            body(0, None, None)
            body(1, 0, None)
            with eng.Fori(0, NB - 2) as i:
                for c, k in counts:
                    c.enter(i, k)
                body(i + 2, i + 1, i)
                for c, k in counts:
                    c.leave(NB - 2, k)
            body(None, NB - 1, NB - 2)
            body(None, None, NB - 1)

        T_USES = 4 + 2 * NP
        T_FREES = 2 + 2 * NP
        M_WRITES = [2 + 2 + 1 + 3 * NP, 2 + 2 + 3 * NP]
        M_READS = [2 + 2 + 1 + 4 * NP, 2 + 2 + 4 * NP]
        CHAIN = IT + 4 + 7
        CONSTS = 12

        block = ctx.enter_context(nc.Block())

        @block.sync
        def _(sp):
            sp.wait_ge(const, 1)
            for dst, src in (
                (w_raw[:, 0:3 * D], dram["wqkv"]),
                (w_raw[:, 3 * D:3 * D + 4 * H], dram["w1p"]),
                (w_raw[:, 3 * D + 4 * H:], dram["w2p"]),
                (wo_raw[:], dram["wout"]),
                (bias[:, 0:3 * D], dram["bqkv"].partition_broadcast(P)),
                (bout[:], dram["bout"].partition_broadcast(P)),
                (pscale[:], dram["scale"].partition_broadcast(P)),
            ):
                sp.dma_start(dst, src).then_inc(ld, 16)

            def rows(hf, value):
                sp.wait_ge(mt_done, value)
                for hh in range(2):
                    sp.dma_start(qt[HP * hh + K - 1:HP * hh + K, 4 * hf:4 * hf + 4, :].bitcast(F32).rearrange("a b (t c) -> a (b t) c", c=P),
                                 mt[4 * IT * hh:4 * IT * (hh + 1), hf, :].bitcast(F32)).then_inc(m_row[hf], 16)

            rows(0, 1)
            with sp.Fori(0, NB - 1) as i:
                rows(1, i * 2 + 2)
                rows(0, i * 2 + 3)
            rows(1, 2 * NB)
            sp.wait_ge(m_row[0], 32 * NB)
            sp.wait_ge(m_row[1], 32 * NB)

        @block.gpsimd
        def _(pool):
            nc.gpsimd.memset(bias[:], 0.0).then_inc(const, 1)
            links = 1

            def link(ins):
                nonlocal links
                links += 1
                ins.then_inc(const, 1)
                pool.wait_ge(const, links)

            nc.gpsimd.memset(qcat[:], 0.0).then_inc(const, 1)
            nc.gpsimd.memset(mx[:], 0.0).then_inc(const, 1)
            links += 2
            link(nc.gpsimd.memset(kcat[:], 0.0))
            link(nc.gpsimd.memset(kcat[:, :, K - 1:K], -1.0))
            link(nc.gpsimd.memset(v_sb[:], 0.0))
            link(nc.gpsimd.memset(v_sb[:, :, DH:DH + 1], 1.0))
            link(nc.gpsimd.memset(causal[:], 0.0))
            link(nc.gpsimd.affine_select(out=causal[:, BANK - P:], in_=causal[:, BANK - P:], compare_op=ALU.is_ge,
                                         fill=-3.0e38, base=0, pattern=[[-1, P]], channel_multiplier=1))
            link(nc.gpsimd.memset(sign[:], 1.0))
            link(nc.gpsimd.memset(sign[:, 1:2], -1.0))
            link(nc.gpsimd.memset(sign[:, 4:5], -1.0))
            assert links == CONSTS
            s_n = Count()

            def exponentiated():
                pool.wait_ge(s_free, s_n.step())
                i = (s_n.local - 1) % (3 * NP)
                nc.gpsimd.tensor_tensor(gate_pool[:, i:i + 1], ident[:, 0:1], ident[:, 0:1], ALU.add)

            def keep(view, blocks):
                return nc.gpsimd.affine_select(out=view, in_=view, compare_op=ALU.is_ge, fill=0.0, base=0,
                                               pattern=[[0, blocks]] * (blocks > 1) + [[1, P]], channel_multiplier=-1)

            def body(c, b, d):
                if c is not None:
                    pool.wait_ge(xn_done, c + 1)
                    xv = x_sb[:, bass.ds(c * IT, IT), :]
                    nc.gpsimd.tensor_tensor(xv, xv, bout[:].unsqueeze(1).to_broadcast([P, IT, D]),
                                            ALU.add).then_inc(bout_added, 1)
                if b is None:
                    return
                for p in range(NP):
                    pr = probs[:, p % 2, :]
                    for h in range(2):
                        exponentiated()
                        o = 2 * BANK * h
                        keep(pr[:, o:o + P], 1)
                        keep(pr[:, o + BANK:o + BANK + 2 * P].rearrange("p (a c) -> p a c", a=2), 2).then_inc(masked, 1)
                    exponentiated()
                    g = pr[:, 4 * BANK:].rearrange("p (a c) -> p a c", a=2)[:, :, 0:P]
                    keep(g, 2).then_inc(masked, 1)

            pool.wait_ge(ld, 16 * 7)
            pipeline(pool, body, [(s_n, 3 * NP)])

        @block.scalar
        def _(act):
            act.wait_ge(var_done, 1)
            nc.scalar.activation(rstd[:], var[:], ACT.Ln).then_inc(rstd_done, 1)
            act.wait_ge(rstd_done, 1)
            nc.scalar.activation(rstd[:], rstd[:], ACT.Exp, scale=-0.5).then_inc(rstd_done, 1)
            t_n, s_n, g_n, pv_n = Count(), Count(), Count(), Count()

            def group(p, g, b):
                n = s_n.now()
                act.wait_ge(s_full, n + 1)
                if g == 0:
                    wait(act, pv_done, pv_n.now() - 1)
                    pv_n.step()
                src = S[(3 * p + g) % 2]
                dst = probs[:, p % 2, :]
                if g < 2:
                    out, in_ = dst[:, 2 * BANK * g:2 * BANK * (g + 1)], src.rearrange("p a c -> p (a c)")
                else:
                    out, in_ = dst[:, 4 * BANK:].rearrange("p (a c) -> p a c", a=2), src[:, :, 0:BANK // 2]
                nc.scalar.activation(out, in_, ACT.Exp).then_inc(s_free, 1)
                s_n.step()

            def take(dst, needed):
                act.wait_ge(t_full, t_n.step())
                wait(act, s_full, needed)
                nc.scalar.copy(dst, T).then_inc(t_free, 1)

            def high(dst):
                act.wait_ge(t_full, t_n.step())
                nc.scalar.copy(dst, T).then_inc(t_half, 1)

            def pv_out(g):
                act.wait_ge(pv_done, g_n.step(2))
                nc.scalar.copy(ao_t[:, g, :], PV).then_inc(pv_free, 1)

            def body(c, b, d):
                if d is not None:
                    pv_out(3)
                if b is not None:
                    t_n.step()
                    for g in range(3):
                        group(0, g, b)
                    first = s_n.now()
                if c is not None:
                    high(xt_hi[:])
                if b is not None:
                    for g in range(3):
                        group(1, g, b)
                if d is not None:
                    high(aot_hi[:])
                for p in range(2, NP):
                    if b is not None and p in (3, 5, 7):
                        pv_out((p - 3) // 2)
                    pairs = (2 * (p - 4), 2 * (p - 4) + 1) if c is not None and p >= 4 else ()

                    def needed(a):
                        return 0 if b is None else first + 3 * a

                    if pairs:
                        take(qt[:, pairs[0], :], needed(pairs[0]))
                    if b is not None:
                        group(p, 0, b)
                    if pairs:
                        take(kt[:, pairs[0], :], needed(pairs[0]))
                    if b is not None:
                        group(p, 1, b)
                        group(p, 2, b)
                    if pairs:
                        take(qt[:, pairs[1], :], needed(pairs[1]))
                        take(kt[:, pairs[1], :], needed(pairs[1]))
                    if c is not None and p == 6:
                        t_n.step()
                    if c is not None and p == 2:
                        act.wait_ge(ss_done, c + 1)
                        nc.scalar.activation(rn[:], ss[:], ACT.Ln, scale=float(2 ** LN_SCALE)).then_inc(rn_done, 1)
                        act.wait_ge(rn_done, c * 2 + 1)
                        nc.scalar.activation(rn[:], rn[:], ACT.Exp, scale=-0.5, bias=half_ln[:]).then_inc(rn_done, 1)

            pipeline(act, body, [(t_n, T_USES), (s_n, 3 * NP), (g_n, NP), (pv_n, NP)])

        @block.vector
        def _(dve):
            chain = Count()

            def link(ins):
                ins.then_inc(link_dve, 1)
                dve.wait_ge(link_dve, chain.step())

            nc.vector.memset(half_ln[:], 0.5 * LN_SCALE * math.log(2.0))
            for t in range(NT):
                last = nc.vector.bn_stats(stats[:, t, :], x_sb[:, t, :])
            link(last)
            for t in range(NT):
                last = nc.vector.bn_aggr(mv[:, t, :], stats[:, t, :])
            link(last)
            nc.vector.tensor_scalar(var[:], mv[:, :, 1], EPS, None, ALU.add).then_inc(var_done, 1)
            dve.wait_ge(ld, 16 * 7)
            link(nc.vector.tensor_copy(w_hi[:], w_raw[:]))
            nc.vector.tensor_tensor(w_lo[:], w_raw[:], w_hi[:].bitcast(F32), ALU.subtract).then_inc(w_done, 1)
            link(nc.vector.tensor_copy(wo_hi[:], wo_raw[:]))
            nc.vector.tensor_tensor(wo_lo[:], wo_raw[:], wo_hi[:].bitcast(F32), ALU.subtract).then_inc(w_done, 1)

            def refine(r, v, t):
                link(nc.vector.tensor_tensor(t, r, r, ALU.mult))
                link(nc.vector.tensor_tensor(t, t, v, ALU.mult))
                link(nc.vector.tensor_scalar(t, t, -0.5, 1.5, ALU.mult, ALU.add))
                link(nc.vector.tensor_tensor(r, r, t, ALU.mult))

            dve.wait_ge(rstd_done, 2)
            refine(rstd[:], var[:], newton[:])
            dve.wait_ge(const, CONSTS)

            t_n, half_n, m_n, m_r = Count(), Count(), [Count(), Count()], [Count(), Count()]
            p1 = raw[:, :, 3 * D:3 * D + 4 * H].rearrange("p i (h k) -> p i h k", k=4)
            p2 = raw[:, :, 3 * D + 4 * H:].rearrange("p i (h k) -> p i h k", k=4)

            def heads(ap):
                return ap.rearrange("p (i h) k -> p i h k", h=H)

            def filled(i):
                dve.wait_ge(m_full[i], m_n[i].step())

            def release(i, ins):
                m_r[i].step()
                return ins.then_inc(m_free[i], 1)

            def maxima_out(hf, c):
                dve.wait_ge(t_full, t_n.step())
                wait(dve, m_row[hf], c * 32)
                nc.vector.tensor_copy(mt[:, hf, :], T[0:2 * 4 * IT, 0:P]).then_inc(mt_done, 1)

            def low(dst, hi):
                t_n.step()
                dve.wait_ge(t_half, half_n.step())
                nc.vector.tensor_tensor(dst, T, hi.bitcast(F32), ALU.subtract).then_inc(t_free, 1)

            def normalise(c):
                for s in range(IT):
                    t = c * IT + s
                    last = nc.vector.tensor_scalar(
                        xn[:, P * s:P * (s + 1)], x_sb[:, bass.ds(t, 1), :].rearrange("p a d -> p (a d)"),
                        mv[:, bass.ds(t, 1), 0], rstd[:, bass.ds(t, 1)], ALU.subtract, ALU.mult)
                last.then_inc(xn_done, 1)

            def divide(it):
                i = it % 2
                filled(i)
                o = M[i].rearrange("p (h k) -> p h k", k=VW)
                link(nc.vector.reciprocal(rec[:, i, :], o[:, :, DH]))
                release(i, nc.vector.tensor_tensor(ao[:, it, :].rearrange("p (h k) -> p h k", k=DH), o[:, :, 0:DH],
                                                   rec[:, i, :].unsqueeze(2).to_broadcast([P, H, DH]), ALU.mult))

            def lines(c):
                for x, y, out in ((p1, p2, heads(la[:])), (p2, p1, heads(lb[:]))):
                    for i, o in ((0, 0), (1, 3), (2, 5)):
                        w = 3 - i
                        last = nc.vector.tensor_tensor(out[:, :, :, o:o + w], y[:, :, :, i + 1:4],
                                                       x[:, :, :, i:i + 1].to_broadcast([P, IT, H, w]), ALU.mult)
                link(last)
                link(nc.vector.tensor_tensor(la[:], la[:], lb[:], ALU.subtract))
                link(nc.vector.tensor_tensor(lb[:], la[:], la[:], ALU.mult))
                link(nc.vector.reduce_sum(ss[:], lb[:], AX_X))
                nc.vector.tensor_scalar(ss[:], ss[:], 1e-24, None, ALU.max).then_inc(ss_done, 1)

            def operands(c):
                nc.vector.tensor_scalar(heads(qf[:])[:, :, :, 0:DH], raw[:, :, 0:D].rearrange("p i (h k) -> p i h k", k=DH),
                                        QSCALE, None, ALU.mult)
                nc.vector.tensor_copy(heads(kf[:])[:, :, :, 0:DH], raw[:, :, D:2 * D].rearrange("p i (h k) -> p i h k", k=DH))
                dve.wait_ge(rn_done, c * 2 + 2)
                refine(rn[:], ss[:], nw[:])
                shape = [P, IT * H, NC]
                link(nc.vector.tensor_tensor(lb[:], la[:], rn[:].unsqueeze(2).to_broadcast(shape), ALU.mult))
                nc.vector.tensor_tensor(kf[:, :, DH:C][:, :, ::-1], lb[:], sign[:].unsqueeze(1).to_broadcast(shape), ALU.mult)
                link(nc.vector.tensor_tensor(heads(qf[:])[:, :, :, DH:C], heads(lb[:]),
                                             pscale[:].unsqueeze(1).unsqueeze(3).to_broadcast([P, IT, H, NC]), ALU.mult))
                nc.vector.tensor_copy(qcat[:, :, 0:2 * C].bitcast(F32R).rearrange("p a (t c) -> p a t c", c=C),
                                      qf[:].unsqueeze(2).to_broadcast([P, IT * H, 2, C]))
                link(nc.vector.tensor_copy(kcat[:, :, 0:C].bitcast(F32R), kf[:]))
                nc.vector.tensor_copy(kcat[:, :, 2 * C:3 * C].bitcast(F32R), kf[:])
                nc.vector.tensor_tensor(qcat[:, :, 2 * C:3 * C].bitcast(F32R), qf[:], qcat[:, :, 0:C], ALU.subtract)
                nc.vector.tensor_tensor(kcat[:, :, C:2 * C].bitcast(F32R), kf[:], kcat[:, :, 0:C],
                                        ALU.subtract).then_inc(cats_done, 1)

            def row_max(a, hh, it):
                w = P * (it + 1)
                o = P if it == 1 else 0
                release(hh, nc.vector.tensor_tensor_reduce(
                    out=junk[:, hh, o:o + w], in0=M[hh][:, o:o + w], in1=causal[:, BANK - w:], scale=1.0, scalar=-3.0e38,
                    op0=ALU.add, op1=ALU.max, accum_out=mx[:, a // 4, hh, a % 4, it:it + 1]))

            def body(c, b, d):
                if c is not None:
                    normalise(c)
                if b is not None:
                    maxima_out(1, b)
                if d is not None:
                    for it in range(IT):
                        divide(it)
                if c is not None:
                    low(xt_lo[:], xt_hi[:])
                    for it in range(IT):
                        filled(it % 2)
                        release(it % 2, nc.vector.tensor_tensor(raw[:, it, :], M[it % 2], bias[:], ALU.add))
                if d is not None:
                    low(aot_lo[:], aot_hi[:])
                if c is not None:
                    link_raw = m_r[1].now()
                    dve.wait_ge(m_free[0], m_r[0].now())
                    dve.wait_ge(m_free[1], link_raw)
                    lines(c)
                    operands(c)
                if d is not None:
                    filled(0)
                    dve.wait_ge(bout_added, d + 1)
                    xv = x_sb[:, bass.ds(d * IT, IT), :]
                    release(0, nc.vector.tensor_tensor(xv, M[0].rearrange("p (a d) -> p a d", d=D), xv, ALU.add))
                if c is not None:
                    for a in range(NP):
                        if a == 6:
                            t_n.step(12)
                            maxima_out(0, c)
                            t_n.step(4)
                        for k, its in enumerate(((0, 1), (2,), (3,))):
                            for hh in range(2):
                                filled(hh)
                                at = (a * 3 + k) * 2 + hh
                                nc.vector.memset(gate_dve[:, at:at + 1], 0.0)
                                for it in its:
                                    row_max(a, hh, it)
                    if b is not None:
                        dve.wait_ge(pv_done, pv_n.step(NP))
                    nc.vector.tensor_copy(heads(v_sb[:])[:, :, :, 0:DH],
                                          raw[:, :, 2 * D:3 * D].rearrange("p i (h k) -> p i h k", k=DH)).then_inc(v_done, 1)

            pv_n = Count()
            pipeline(dve, body, [(t_n, T_USES), (half_n, 2), (m_n[0], M_WRITES[0]), (m_n[1], M_WRITES[1]),
                                 (m_r[0], M_READS[0]), (m_r[1], M_READS[1]), (chain, CHAIN), (pv_n, NP)])

        @block.tensor
        def _(pe):
            t_n, t_r, mt_n, s_n, pv_n, g_n = Count(), Count(), Count(), Count(), Count(), Count()
            m_r = [Count(), Count()]
            freed = [None]

            def product(out, a_hi, a_lo, b_hi, b_lo):
                nc.tensor.matmul(out, a_hi, b_hi, start=True, stop=False)
                nc.tensor.matmul(out, a_hi, b_lo, start=False, stop=False)
                return nc.tensor.matmul(out, a_lo, b_hi, start=False, stop=True)

            def transposes(pieces, maxima=False):
                pe.wait_ge(t_free, t_r.now()) if not (isinstance(t_r.now(), int) and t_r.now() == 0) else None
                wait(pe, mt_done, mt_n.now())
                for dst, src in pieces:
                    last = nc.tensor.transpose(dst, src, ident[:])
                last.then_inc(t_full, 1)
                (mt_n if maxima else t_r).step()

            def bank(i, reads):
                wait(pe, m_free[i], m_r[i].now())
                m_r[i].step(reads)

            def maxima(hf):
                for i in range(2):
                    wait(pe, m_free[i], m_r[i].now())
                transposes([(T[0:2 * 4 * IT, 0:P], mx[:, hf, :, :, :].rearrange("p a b c -> p (a b c)"))], maxima=True)

            def pair(cat, a):
                return [(T[:, P * it:P * (it + 1)],
                         cat[:, H * it + 2 * a:H * it + 2 * a + 2, :].rearrange("p a c -> p (a c)")) for it in range(IT)]

            def logits(p, g):
                n = s_n.step()
                wait(pe, s_free, n - 2)
                s = S[(3 * p + g) % 2]

                def one(hh, jt, out):
                    r = slice(HP * hh, HP * hh + K)
                    return nc.tensor.matmul(out, kt[r, p, P * jt:P * (jt + 1)], qt[r, p, P * jt:], start=True, stop=True)

                if g < 2:
                    one(g, 0, s[:, 0, :])
                    one(g, 3, s[:, 1, 0:P])
                    one(g, 1, s[:, 1, P:]).then_inc(s_full, 1)
                else:
                    one(0, 2, s[:, 0, 0:2 * P])
                    one(1, 2, s[:, 1, 0:2 * P]).then_inc(s_full, 1)

            def values(p, part):
                hh = part // 2
                h = 2 * p + hh
                out = PV[VW * (h % 4):VW * (h % 4 + 1), :]
                pr = probs[:, p % 2, :]
                if part == 0:
                    pe.wait_ge(masked, pv_n.now() * 3 + 3)
                    if p % 2 == 0:
                        wait(pe, pv_free, g_n.now())
                        g_n.step()
                if part % 2 == 0:
                    nc.tensor.matmul(out, v_sb[:, h, :], pr[:, 2 * BANK * hh:2 * BANK * hh + BANK], start=True, stop=False)
                    return
                for jt, at in ((1, 2 * BANK * hh + BANK + P), (2, 4 * BANK + 2 * P * hh), (3, 2 * BANK * hh + BANK)):
                    last = nc.tensor.matmul(out[:, P * jt:], v_sb[:, H * jt + h, :], pr[:, at:at + BANK - P * jt],
                                            start=False, stop=jt == 3)
                if part == 3:
                    last.then_inc(pv_done, 1)
                    pv_n.step()

            def row_logits(a, part):
                for hh in range(2):
                    bank(hh, 2 if part == 0 else 1)
                    r = slice(HP * hh, HP * hh + K)
                    for it in (0, 1) if part == 0 else (part + 1,):
                        w = P * (it + 1)
                        o = P if it == 1 else 0
                        last = nc.tensor.matmul(M[hh][:, o:o + w], qt[r, a, P * it:P * (it + 1)], kt[r, a, 0:w],
                                                start=True, stop=True)
                    last.then_inc(m_full[hh], 1)

            def project(c, it):
                bank(it % 2, 1)
                t = slice(P * it, P * (it + 1))
                product(M[it % 2], xt_hi[:, t], xt_lo[:, t], w_hi[:], w_lo[:]).then_inc(m_full[it % 2], 1)

            def body(c, b, d):
                if b is not None:
                    pe.wait_ge(m_row[0], b * 32 + 32)
                    logits(0, 0)
                    logits(0, 1)
                    maxima(1)
                    logits(0, 2)
                if c is not None:
                    pe.wait_ge(xn_done, c + 1)
                    transposes([(T[:, P * s:P * (s + 1)], xn[:, P * s:P * (s + 1)]) for s in range(IT)])
                if d is not None:
                    pe.wait_ge(pv_free, d * 4 + 4)
                    for it in range(IT):
                        bank(it % 2, 1)
                        for g in range(H // 4):
                            last = nc.tensor.transpose(M[it % 2][:, P * g:P * (g + 1)], ao_t[:, g, P * it:P * (it + 1)], ident[:])
                        last.then_inc(m_full[it % 2], 1)
                if c is not None:
                    pe.wait_ge(w_done, 1)
                    pe.wait_ge(t_free, t_r.now())
                if b is not None:
                    for g in range(3):
                        logits(1, g)
                    pe.wait_ge(v_done, b + 1)
                for it in range(IT):
                    if c is not None:
                        project(c, it)
                    if b is not None:
                        values(0, it)
                if d is not None:
                    for i in range(2):
                        pe.wait_ge(m_free[i], m_r[i].now() - (0 if c is None else 2))
                    transposes([(T[:, P * it:P * (it + 1)], ao[:, it, :]) for it in range(IT)])
                if b is not None:
                    for p in (2, 3):
                        for g in range(3):
                            logits(p, g)
                        for part in range(4):
                            if p == 3 and part == 2 and d is not None:
                                out_project()
                            values(p - 1, part)
                elif d is not None:
                    out_project()
                if c is not None:
                    pe.wait_ge(cats_done, c + 1)
                for p in range(4, NP):
                    a = 2 * (p - 4)
                    if b is not None and p == 4:
                        pe.wait_ge(m_row[1], b * 32 + 32)
                    if c is not None:
                        if p == 7:
                            maxima(0)
                        transposes(pair(qcat, a))
                    if b is not None:
                        logits(p, 0)
                    if c is not None:
                        transposes(pair(kcat, a))
                    if b is not None:
                        logits(p, 1)
                        values(p - 1, 0)
                    if c is not None:
                        pe.wait_ge(t_free, t_r.now())
                        row_logits(a, 0)
                    if b is not None:
                        values(p - 1, 1)
                        logits(p, 2)
                    if c is not None:
                        row_logits(a, 1)
                        row_logits(a, 2)
                        transposes(pair(qcat, a + 1))
                    if b is not None:
                        values(p - 1, 2)
                    if c is not None:
                        transposes(pair(kcat, a + 1))
                    if b is not None:
                        values(p - 1, 3)
                    if c is not None:
                        pe.wait_ge(t_free, t_r.now())
                        for part in range(3):
                            row_logits(a + 1, part)
                if b is not None:
                    for part in range(4):
                        values(NP - 1, part)

            def out_project():
                pe.wait_ge(w_done, 2)
                pe.wait_ge(t_free, t_r.now())
                bank(0, 1)
                for it in range(IT):
                    t = slice(P * it, P * (it + 1))
                    last = product(M[0][:, P * it:P * (it + 1)], aot_hi[:, t], aot_lo[:, t], wo_hi[:], wo_lo[:])
                last.then_inc(m_full[0], 1)

            pipeline(pe, body, [(t_r, T_FREES), (mt_n, 2), (s_n, 3 * NP), (pv_n, NP), (g_n, NP // 2),
                                (m_r[0], M_READS[0]), (m_r[1], M_READS[1])])


def ffn_phase(nc, tag, psum, x_sb, ident, dram, x_in, y_out):
    NT = x_sb.shape[1]
    D = x_sb.shape[2]
    TOK = NT * P
    NE, _, F = dram["w_gate"].shape
    FC = F // P
    TT = TOK // BANK
    SUB = BANK // P
    NR = 2 * NE
    WCOLS = 3 * F
    CHUNK = WCOLS // TT
    HALF = TOK // 2
    assert D == P and FC == 4 and NE % 2 == 0 and WCOLS % TT == 0 and NT * NR == BANK

    with ExitStack() as ctx:
        def sb(name, shape, dt=F32):
            return ctx.enter_context(nc.sbuf_tensor(f"{name}_{tag}", shape, dt))

        def sem(name):
            return ctx.enter_context(nc.semaphore(f"{name}_{tag}"))

        xt_hi = sb("xt_hi", [P, TOK], F32R)
        xt_lo = sb("xt_lo", [P, TOK], F32R)
        f_acc = sb("f_acc", [P, TOK])
        w_raw = sb("w_raw", [P, 2, WCOLS])
        w_hi = sb("w_hi", [P, 2, WCOLS], F32R)
        w_lo = sb("w_lo", [P, 2, WCOLS], F32R)
        wr_raw = sb("wr_raw", [P, P])
        wr_hi = sb("wr_hi", [P, P], F32R)
        wr_lo = sb("wr_lo", [P, P], F32R)
        xn = sb("xn", [P, 2, BANK])
        stats = sb("stats", [P, NT, 6])
        mv = sb("mv", [P, NT, 2])
        rstd = sb("rstd", [P, NT])
        var = sb("var", [P, NT])
        newton = sb("newton", [P, NT])
        logit_t = sb("logit_t", [NR, TOK])
        probs = sb("probs", [P, NT, 2, NE])
        red = sb("red", [P, NT * 2])
        cw = sb("cw", [P, 2, NE, NT // 2])
        cws = sb("cws", [P, NT])
        cw_rows = sb("cw_rows", [P, 2, P])
        cwb = sb("cwb", [P, 2, TOK])
        s_buf = sb("s_buf", [P, 2, BANK])
        h_buf = sb("h_buf", [P, 2, BANK])
        h_hi = sb("h_hi", [P, FC, BANK], F32R)
        h_lo = sb("h_lo", [P, FC, BANK], F32R)
        o_tmp = sb("o_tmp", [P, BANK])

        x_ld = [sem(f"x_ld{i}") for i in range(TT)]
        w_ld = [sem(f"w_ld{i}") for i in range(2)]
        cwb_ld = [sem(f"cwb_ld{i}") for i in range(2)]
        wr_ld = sem("wr_ld")
        wr_zero = sem("wr_zero")
        f_zero = sem("f_zero")
        dve_link = sem("dve_link")
        var_done = sem("var_done")
        std_done = sem("std_done")
        xn_done = sem("xn_done")
        xt_tr = sem("xt_tr")
        xt_hi_done = sem("xt_hi_done")
        xt_lo_done = sem("xt_lo_done")
        w0_hi = sem("w0_hi")
        w0_done = sem("w0_done")
        wr_done = sem("wr_done")
        logit_mm = sem("logit_mm")
        logit_cp = sem("logit_cp")
        logit_tr = sem("logit_tr")
        shifted = sem("shifted")
        exp_done = sem("exp_done")
        cw_done = sem("cw_done")
        cw_tr = sem("cw_tr")
        cw_cp = sem("cw_cp")
        cw_st = sem("cw_st")
        gu_done = sem("gu_done")
        silu_done = sem("silu_done")
        h_done = sem("h_done")
        hi_done = sem("hi_done")
        lo_done = sem("lo_done")
        down_done = sem("down_done")
        o_read = sem("o_read")
        o_added = sem("o_added")
        w_chunk = sem("w_chunk")
        w_chunk_hi = sem("w_chunk_hi")
        f_tr = sem("f_tr")
        x_new = sem("x_new")
        y_st = sem("y_st")

        G = [psum[:, 0, :], psum[:, 1, :]]
        U = [psum[:, 2, :], psum[:, 3, :]]
        def O(t):
            return psum[:, bass.ds(4 + t % 2, 1), :].rearrange("p a c -> p (a c)")

        XT = [psum[:, 6, :], psum[:, 7, :]]
        LT = [psum[:, 4, :], psum[:, 5, :]]
        LG = psum[:, 6, :]
        CT = psum[:, 7, 0:2 * P]
        FT = [psum[:, 6, :], psum[:, 7, :]]

        def wait(eng, s, value):
            if not (isinstance(value, int) and value <= 0):
                eng.wait_ge(s, value)

        def over_tiles(eng, tile):
            tile(0, 0, 0, 0, None)
            with eng.Fori(1, TT) as t:
                tile(t, 0, t, 0, 0)
            with eng.Fori(0, NE // 2 - 1) as m:
                for d in (1, 2):
                    e = 2 * m + d
                    n0 = m * (2 * TT) + TT * d
                    tile(n0, e, 0, d % 2, 0 if d == 1 else 2)
                    with eng.Fori(1, TT) as t:
                        tile(n0 + t, e, t, d % 2, 1)
            e = NE - 1
            tile(TT * e, e, 0, 1, 2)
            with eng.Fori(1, TT) as t:
                tile(t + TT * e, e, t, 1, 1)

        block = ctx.enter_context(nc.Block())

        @block.sync
        def _(sp):
            if x_in is not None:
                x_view = x_in.rearrange("(t p) d -> p t d", p=P)
                for j in range(TT):
                    sp.dma_start(x_sb[:, SUB * j:SUB * (j + 1), :],
                                 x_view[:, SUB * j:SUB * (j + 1), :]).then_inc(x_ld[j], 16)

            def load_expert(e, par):
                sp.dma_start(w_raw[:, par, 0:F],
                             dram["w_gate"][bass.ds(e, 1)].rearrange("a k f -> k (a f)")).then_inc(w_ld[par], 16)
                sp.dma_start(w_raw[:, par, F:2 * F],
                             dram["w_up"][bass.ds(e, 1)].rearrange("a k f -> k (a f)")).then_inc(w_ld[par], 16)
                sp.dma_start(w_raw[:, par, 2 * F:].rearrange("p (c h) -> p c h", c=FC),
                             dram["w_down"][bass.ds(e, 1)].rearrange("a (c p) h -> p (a c) h",
                                                                     p=P)).then_inc(w_ld[par], 16)

            def load_cw(e, par):
                for c in range(2):
                    sp.dma_start(cwb[:, par, HALF * c:HALF * (c + 1)],
                                 dram["cw_rows_" + tag][c, bass.ds(e, 1), :].partition_broadcast(P)
                                 ).then_inc(cwb_ld[par], 16)

            sp.wait_ge(wr_zero, 1)
            sp.dma_start(wr_raw[:, 0:NE], dram["w_router"]).then_inc(wr_ld, 16)
            sp.dma_start(wr_raw[:, NE:NR], dram["w_gating"]).then_inc(wr_ld, 16)
            load_expert(0, 0)
            load_expert(1, 1)
            sp.wait_ge(cw_cp, 1)
            for c in range(2):
                sp.dma_start(dram["cw_rows_" + tag][c].rearrange("e (t p) -> (e t) p", p=P),
                             cw_rows[:, c, :]).then_inc(cw_st, 16)
            sp.wait_ge(cw_st, 32)
            load_cw(0, 0)
            load_cw(1, 1)
            sp.wait_ge(w0_done, 1)
            load_expert(2, 0)
            sp.wait_ge(o_read, TT + 1)
            load_cw(2, 0)
            with sp.Fori(0, (NE - 4) // 2) as m:
                for d in (3, 4):
                    e = 2 * m + d
                    sp.wait_ge(w_chunk, m * (2 * TT) + TT * (d - 2))
                    load_expert(e, d % 2)
                    sp.wait_ge(o_read, m * (2 * TT) + (TT * (d - 1) + 1))
                    load_cw(e, d % 2)
            e = NE - 1
            sp.wait_ge(w_chunk, TT * (e - 2))
            load_expert(e, 1)
            sp.wait_ge(o_read, TT * (e - 1) + 1)
            load_cw(e, 1)
            if y_out is not None:
                y_view = y_out.rearrange("(t p) d -> p t d", p=P)
                for j in range(TT):
                    sp.wait_ge(x_new, j + 1)
                    sp.dma_start(y_view[:, SUB * j:SUB * (j + 1), :],
                                 x_sb[:, SUB * j:SUB * (j + 1), :]).then_inc(y_st, 16)
                sp.wait_ge(y_st, 16 * TT)

        @block.gpsimd
        def _(pool):
            nc.gpsimd.memset(wr_raw[:], 0.0).then_inc(wr_zero, 1)
            nc.gpsimd.memset(f_acc[:], 0.0).then_inc(f_zero, 1)

            def low_part(q, f):
                pool.wait_ge(hi_done, q + 1)
                nc.gpsimd.tensor_tensor(h_lo[:, f, :], h_buf[:, f % 2, :], h_hi[:, f, :].bitcast(F32),
                                        ALU.subtract).then_inc(lo_done, 1)

            with pool.Fori(0, TT * NE) as n:
                for f in range(FC):
                    low_part(n * FC + f, f)

        @block.scalar
        def _(act):
            act.wait_ge(w_ld[0], 48)
            nc.scalar.copy(w_hi[:, 0, :], w_raw[:, 0, :]).then_inc(w0_hi, 1)
            act.wait_ge(var_done, 1)
            nc.scalar.activation(rstd[:], var[:], ACT.Ln).then_inc(std_done, 1)
            act.wait_ge(std_done, 1)
            nc.scalar.activation(rstd[:], rstd[:], ACT.Exp, scale=-0.5).then_inc(std_done, 1)
            with act.Fori(0, TT // 2) as i:
                for b in range(2):
                    j = i * 2 + b
                    act.wait_ge(xt_tr, j + 1)
                    nc.scalar.copy(xt_hi[:, bass.ts(j, BANK)], XT[b]).then_inc(xt_hi_done, 1)
            with act.Fori(0, TT // 2) as i:
                for b in range(2):
                    j = i * 2 + b
                    act.wait_ge(logit_mm, j + 1)
                    nc.scalar.copy(logit_t[:, bass.ts(j, BANK)], LT[b][0:NR, :]).then_inc(logit_cp, 1)
            act.wait_ge(shifted, 1)
            nc.scalar.activation(probs[:, :, 0, :], probs[:, :, 0, :], ACT.Exp).then_inc(exp_done, 1)
            nc.scalar.activation(probs[:, :, 1, :], probs[:, :, 1, :], ACT.Exp, scale=10.0).then_inc(exp_done, 1)

            def silu(q, f):
                act.wait_ge(gu_done, q + 1)
                wait(act, h_done, q - 1)
                nc.scalar.activation(s_buf[:, f % 2, :], G[f % 2], ACT.Silu).then_inc(silu_done, 1)

            def high_part(q, f):
                act.wait_ge(h_done, q + 1)
                wait(act, down_done, q - (FC - 1))
                nc.scalar.copy(h_hi[:, f, :], h_buf[:, f % 2, :]).then_inc(hi_done, 1)

            def tile(n, e, t, par, prev):
                for f in range(FC):
                    q = n * FC + f
                    silu(q, f)
                    high_part(q, f)

            over_tiles(act, tile)

        @block.vector
        def _(dve):
            links = [0]

            def link(ins):
                links[0] += 1
                ins.then_inc(dve_link, 1)
                dve.wait_ge(dve_link, links[0])

            nc.vector.engine_nop().then_inc(o_read, 1)
            nc.vector.engine_nop().then_inc(o_added, 1)
            for t in range(NT):
                if x_in is not None and t % SUB == 0:
                    dve.wait_ge(x_ld[t // SUB], 16)
                last = nc.vector.bn_stats(stats[:, t, :], x_sb[:, t, :])
            link(last)
            for t in range(NT):
                last = nc.vector.bn_aggr(mv[:, t, :], stats[:, t, :])
            link(last)
            nc.vector.tensor_scalar(var[:], mv[:, :, 1], EPS, None, ALU.add).then_inc(var_done, 1)
            dve.wait_ge(w0_hi, 1)
            nc.vector.tensor_tensor(w_lo[:, 0, :], w_raw[:, 0, :], w_hi[:, 0, :].bitcast(F32),
                                    ALU.subtract).then_inc(w0_done, 1)
            dve.wait_ge(wr_ld, 32)
            link(nc.vector.tensor_copy(wr_hi[:], wr_raw[:]))
            nc.vector.tensor_tensor(wr_lo[:], wr_raw[:], wr_hi[:].bitcast(F32), ALU.subtract).then_inc(wr_done, 1)
            dve.wait_ge(std_done, 2)
            link(nc.vector.tensor_tensor(newton[:], rstd[:], rstd[:], ALU.mult))
            link(nc.vector.tensor_tensor(newton[:], newton[:], var[:], ALU.mult))
            link(nc.vector.tensor_scalar(newton[:], newton[:], -0.5, 1.5, ALU.mult, ALU.add))
            link(nc.vector.tensor_tensor(rstd[:], rstd[:], newton[:], ALU.mult))

            def normalise(j, b):
                wait(dve, xt_tr, j - 1)
                for s in range(SUB):
                    t = j * SUB + s
                    last = nc.vector.tensor_scalar(xn[:, b, P * s:P * (s + 1)], x_sb[:, bass.ds(t, 1), :].rearrange("p a d -> p (a d)"),
                                                   mv[:, bass.ds(t, 1), 0], rstd[:, bass.ds(t, 1)],
                                                   ALU.subtract, ALU.mult)
                last.then_inc(xn_done, 1)

            def low_xt(j, b):
                dve.wait_ge(xt_hi_done, j + 1)
                nc.vector.tensor_tensor(xt_lo[:, bass.ts(j, BANK)], XT[b], xt_hi[:, bass.ts(j, BANK)].bitcast(F32),
                                        ALU.subtract).then_inc(xt_lo_done, 1)

            normalise(0, 0)
            normalise(1, 1)
            with dve.Fori(0, TT // 2 - 1) as i:
                for b in range(2):
                    low_xt(i * 2 + b, b)
                    normalise(i * 2 + b + 2, b)
            low_xt(TT - 2, 0)
            low_xt(TT - 1, 1)

            dve.wait_ge(logit_tr, 1)
            lg = LG.rearrange("p (a e) -> p a e", e=NE)
            pr = probs[:].rearrange("p t s e -> p (t s) e")
            wide = [P, NT * 2, NE]
            link(nc.vector.reduce_max(red[:], lg, AX_X))
            nc.vector.tensor_tensor(pr, lg, red[:].unsqueeze(2).to_broadcast(wide), ALU.subtract).then_inc(shifted, 1)
            dve.wait_ge(exp_done, 2)
            link(nc.vector.reduce_sum(red[:], pr, AX_X))
            link(nc.vector.reciprocal(red[:], red[:]))
            link(nc.vector.tensor_tensor(pr, pr, red[:].unsqueeze(2).to_broadcast(wide), ALU.mult))
            link(nc.vector.tensor_tensor(probs[:, :, 0, :], probs[:, :, 0, :], probs[:, :, 1, :], ALU.mult))
            link(nc.vector.reduce_sum(cws[:], probs[:, :, 0, :], AX_X))
            link(nc.vector.tensor_scalar(cws[:], cws[:], 1e-9, None, ALU.add))
            link(nc.vector.reciprocal(cws[:], cws[:]))
            for c in range(2):
                last = nc.vector.tensor_tensor(
                    cw[:, c, :, :].rearrange("p e t -> p t e"), probs[:, NT // 2 * c:NT // 2 * (c + 1), 0, :],
                    cws[:, NT // 2 * c:NT // 2 * (c + 1)].unsqueeze(2).to_broadcast([P, NT // 2, NE]), ALU.mult)
            last.then_inc(cw_done, 1)

            def multiply(q, f):
                dve.wait_ge(silu_done, q + 1)
                wait(dve, lo_done, q - 1)
                nc.vector.tensor_tensor(h_buf[:, f % 2, :], U[f % 2], s_buf[:, f % 2, :],
                                        ALU.mult).then_inc(h_done, 1)

            def weigh(n, t, par, e):
                dve.wait_ge(cwb_ld[par], 32 * (e // 2 + 1) if isinstance(e, int) else e * 16 + (32 - 16 * par))
                dve.wait_ge(down_done, (n + 1) * FC)
                dve.wait_ge(o_added, n + 1)
                nc.vector.tensor_tensor(o_tmp[:], O(t), cwb[:, par, bass.ts(t, BANK)], ALU.mult).then_inc(o_read, 1)

            def add(n, t):
                dve.wait_ge(o_read, n + 2)
                nc.vector.tensor_tensor(f_acc[:, bass.ts(t, BANK)], f_acc[:, bass.ts(t, BANK)], o_tmp[:],
                                        ALU.add).then_inc(o_added, 1)

            def tile(n, e, t, par, prev):
                split = not (isinstance(e, int) and e == NE - 1)
                new = isinstance(t, int)
                pe, pt, ppar = (e - 1, TT - 1, 1 - par) if new else (e, t - 1, par)
                multiply(n * FC, 0)
                multiply(n * FC + 1, 1)
                if prev is not None:
                    weigh(n - 1, pt, ppar, pe)
                multiply(n * FC + 2, 2)
                if prev is not None:
                    add(n - 1, pt)
                cols = bass.ts(t, CHUNK)
                if split:
                    dve.wait_ge(w_ld[1 - par], 48 * ((e + 1) // 2 + 1) if isinstance(e, int) else e * 24 + (72 - 24 * (1 - par)))
                    nc.vector.tensor_copy(w_hi[:, 1 - par, cols], w_raw[:, 1 - par, cols]).then_inc(w_chunk_hi, 1)
                multiply(n * FC + 3, 3)
                if split:
                    dve.wait_ge(w_chunk_hi, n + 1)
                    nc.vector.tensor_tensor(w_lo[:, 1 - par, cols], w_raw[:, 1 - par, cols],
                                            w_hi[:, 1 - par, cols].bitcast(F32), ALU.subtract).then_inc(w_chunk, 1)
                if isinstance(n, int) and n == 0:
                    dve.wait_ge(cw_tr, 1)
                    nc.vector.tensor_copy(cw_rows[:].rearrange("p c q -> p (c q)"), CT).then_inc(cw_cp, 1)

            dve.wait_ge(f_zero, 1)
            over_tiles(dve, tile)
            last_n = TT * NE - 1
            weigh(last_n, TT - 1, 1, NE - 1)
            add(last_n, TT - 1)

            for j in range(TT):
                dve.wait_ge(f_tr, j + 1)
                xv = x_sb[:, SUB * j:SUB * (j + 1), :].rearrange("p a d -> p (a d)")
                nc.vector.scalar_tensor_tensor(xv, FT[j % 2], 0.5, xv, ALU.mult, ALU.add).then_inc(x_new, 1)

        @block.tensor
        def _(pe):
            def product(out, a_hi, a_lo, b_hi, b_lo, start, stop):
                nc.tensor.matmul(out, a_hi, b_hi, start=start, stop=False)
                nc.tensor.matmul(out, a_hi, b_lo, start=False, stop=False)
                return nc.tensor.matmul(out, a_lo, b_hi, start=False, stop=stop)

            with pe.Fori(0, TT // 2) as i:
                for b in range(2):
                    j = i * 2 + b
                    pe.wait_ge(xn_done, j + 1)
                    for s in range(SUB):
                        last = nc.tensor.transpose(XT[b][:, P * s:P * (s + 1)], xn[:, b, P * s:P * (s + 1)], ident[:])
                    last.then_inc(xt_tr, 1)
            pe.wait_ge(wr_done, 1)

            def router(j, b):
                pe.wait_ge(xt_lo_done, j + 1)
                wait(pe, logit_cp, j - 1)
                cols = bass.ts(j, BANK)
                product(LT[b], wr_hi[:], wr_lo[:], xt_hi[:, cols], xt_lo[:, cols], True, True).then_inc(logit_mm, 1)

            router(0, 0)
            router(1, 1)
            with pe.Fori(1, TT // 2) as i:
                for b in range(2):
                    router(i * 2 + b, b)
            pe.wait_ge(logit_cp, TT)
            for t in range(NT):
                last = nc.tensor.transpose(LG[:, NR * t:NR * (t + 1)], logit_t[:, P * t:P * (t + 1)], ident[0:NR, 0:NR])
            last.then_inc(logit_tr, 1)
            pe.wait_ge(w0_done, 1)

            def gate_up(q, f, t, par):
                wait(pe, h_done, q - 1)
                cols = bass.ts(t, BANK)
                for dst, at in ((G[f % 2], f * P), (U[f % 2], F + f * P)):
                    w = slice(at, at + P)
                    last = product(dst, w_hi[:, par, w], w_lo[:, par, w], xt_hi[:, cols], xt_lo[:, cols], True, True)
                last.then_inc(gu_done, 1)

            def down(q, f, par, n, t):
                pe.wait_ge(lo_done, q + 1)
                if f == 0:
                    wait(pe, o_read, n)
                w = slice(2 * F + f * P, 2 * F + (f + 1) * P)
                product(O(t), w_hi[:, par, w], w_lo[:, par, w], h_hi[:, f, :], h_lo[:, f, :],
                        f == 0, f == FC - 1).then_inc(down_done, 1)

            def tile(n, e, t, par, prev):
                new = isinstance(t, int)
                if new and prev is not None:
                    pe.wait_ge(w_chunk, n)
                ppar = 1 - par if new else par
                for f in range(FC):
                    q = n * FC + f
                    gate_up(q, f, t, par)
                    if f >= 2:
                        down(q - 2, f - 2, par, n, t)
                    elif prev is not None:
                        down(q - 2, f + 2, ppar, n - 1, TT - 1 if new else t - 1)
                if isinstance(n, int) and n == 0:
                    pe.wait_ge(cw_done, 1)
                    for c in range(2):
                        last = nc.tensor.transpose(CT[:, P * c:P * (c + 1)], cw[:, c, :, :].rearrange("p e t -> p (e t)"), ident[:])
                    last.then_inc(cw_tr, 1)

            over_tiles(pe, tile)
            last_q = TT * NE * FC
            down(last_q - 2, 2, 1, TT * NE - 1, TT - 1)
            down(last_q - 1, 3, 1, TT * NE - 1, TT - 1)
            pe.wait_ge(o_added, TT * NE + 1)
            for j in range(TT):
                if j >= 2:
                    pe.wait_ge(x_new, j - 1)
                for s in range(SUB):
                    t = j * SUB + s
                    last = nc.tensor.transpose(FT[j % 2][:, P * s:P * (s + 1)], f_acc[:, P * t:P * (t + 1)], ident[:])
                last.then_inc(f_tr, 1)


def macaron_block(nc, x, wqkv, bqkv, w1p, w2p, scale, wout, bout, w_router, w_gating, w_gate, w_up, w_down, out):
    D = x.shape[2]
    tokens = x.shape[0] * x.shape[1]
    NE = w_gate.shape[0]
    assert x.shape[1] == BANK, "a block of 512 columns is a sequence of the attention"
    x_rows, out_rows = (a.rearrange("b t d -> (b t) d") for a in (x, out))
    ffn = dict(w_router=w_router, w_gating=w_gating, w_gate=w_gate, w_up=w_up, w_down=w_down)
    for tag in ("f1", "f2"):
        ffn["cw_rows_" + tag] = nc.dram_tensor("cw_dram_" + tag, (2, NE, tokens // 2), F32, kind="Internal").ap()
    with ExitStack() as ctx:
        psum = ctx.enter_context(nc.psum_tensor("psum", [P, 8, BANK], F32))
        x_sb = ctx.enter_context(nc.sbuf_tensor("x_sb", [P, tokens // P, D], F32))
        ident = ctx.enter_context(nc.sbuf_tensor("ident", [P, P], F32))
        ident_zero = ctx.enter_context(nc.semaphore("ident_zero"))
        with nc.Block() as block:
            @block.gpsimd
            def _(pool):
                nc.gpsimd.memset(ident[:], 0.0).then_inc(ident_zero, 1)
                pool.wait_ge(ident_zero, 1)
                nc.gpsimd.affine_select(out=ident[:], in_=ident[:], compare_op=ALU.not_equal, fill=1.0, base=0,
                                        pattern=[[-1, P]], channel_multiplier=1).then_inc(ident_zero, 1)
                pool.wait_ge(ident_zero, 2)
        ffn_phase(nc, "f1", psum, x_sb, ident, ffn, x_rows, None)
        attention_phase(nc, psum, x_sb, ident, dict(wqkv=wqkv, bqkv=bqkv, w1p=w1p, w2p=w2p, scale=scale,
                                                    wout=wout, bout=bout))
        ffn_phase(nc, "f2", psum, x_sb, ident, ffn, None, out_rows)


_INS = ["L0_attn_x", "L0_attn_Wqkv", "L0_attn_bqkv", "L0_attn_W1p", "L0_attn_W2p", "L0_attn_plucker_scale",
        "L0_attn_Wout", "L0_attn_bout", "L0_ffn_w_router", "L0_ffn_w_gating", "L0_ffn_w_gate", "L0_ffn_w_up",
        "L0_ffn_w_down"]


def kernel(**inputs):
    import numpy as _np
    import concourse.bacc as _bacc
    from concourse import mybir as _mybir
    from concourse.bass_utils import run_bass_kernel_spmd as _run

    nc = _bacc.Bacc("TRN2", target_bir_lowering=False, num_devices=1)
    arrays, args = {}, []
    for name in _INS:
        a = _np.ascontiguousarray(inputs[name])
        arrays[f"in_{name}_dram"] = a
        args.append(nc.dram_tensor(f"in_{name}_dram", a.shape, _mybir.dt.from_np(a.dtype), kind="ExternalInput").ap())
    out = nc.dram_tensor("out_0_dram", inputs["L0_attn_x"].shape, _mybir.dt.float32, kind="ExternalOutput").ap()
    macaron_block(nc, *args, out)
    r = _run(nc, [arrays], core_ids=[0])
    return r.results[0]["out_0_dram"]
```

```python
from contextlib import ExitStack

import concourse.bass as bass
from concourse import mybir

F32 = mybir.dt.float32
F32R = mybir.dt.float32r
ALU = mybir.AluOpType
ACT = mybir.ActivationFunctionType
AX_X = mybir.AxisListType.X

P = 128
BANK = 512
EPS = 1e-5
RSQRT_MAGIC = float(0x5F3759DF)


class Count:

    def __init__(self):
        self.base, self.local = 0, 0

    def now(self):
        return self.base + self.local

    def step(self, k=1):
        self.local += k
        return self.now()

    def enter(self, i, per_round):
        self.outer = self.base + self.local
        self.base, self.local = self.outer + i * per_round, 0

    def leave(self, rounds, per_round):
        assert self.local == per_round, (self.local, per_round)
        self.base, self.local = self.outer + rounds * per_round, 0


def attention_phase(nc, psum, x_sb, ident, dram):
    NT, D = x_sb.shape[1:]
    H = dram["scale"].shape[0]
    DH = D // H
    NC = 6
    C = DH + NC
    K = 3 * C + 1
    HP = 64
    NP = H // 2
    IT = BANK // P
    NB = NT // IT
    VW = 32
    assert DH == 8 and NP == 8 and K <= HP and NB >= 3
    QSCALE = float(DH) ** -0.5

    with ExitStack() as ctx:
        def sb(name, shape, dt=F32):
            return ctx.enter_context(nc.sbuf_tensor("a_" + name, shape, dt))

        def sem(name):
            return ctx.enter_context(nc.semaphore("a_" + name))

        w_raw = sb("w_raw", [P, BANK])
        w_hi = sb("w_hi", [P, BANK], F32R)
        w_lo = sb("w_lo", [P, BANK], F32R)
        wo_raw = sb("wo_raw", [P, D])
        wo_hi = sb("wo_hi", [P, D], F32R)
        wo_lo = sb("wo_lo", [P, D], F32R)
        bias = sb("bias", [P, BANK])
        bout = sb("bout", [P, D])
        pscale = sb("pscale", [P, H])
        line_scale = sb("line_scale", [P, H, NC])
        causal = sb("causal", [P, BANK])
        stats = sb("stats", [P, NT, 6])
        mv = sb("mv", [P, NT, 2])
        var = sb("var", [P, NT])
        rstd = sb("rstd", [P, NT])
        newton = sb("newton", [P, NT])
        xn = sb("xn", [P, BANK])
        xt_hi = sb("xt_hi", [P, BANK], F32R)
        xt_lo = sb("xt_lo", [P, BANK], F32R)
        raw = sb("raw", [P, IT, BANK])
        la = sb("la", [P, IT * H, NC])
        lb = sb("lb", [P, IT * H, NC])
        ss = sb("ss", [P, IT * H])
        rn = sb("rn", [P, IT * H])
        nw = sb("nw", [P, IT * H])
        qf = sb("qf", [P, IT * H, C])
        kf = sb("kf", [P, IT * H, C])
        qcat = sb("qcat", [P, IT * H, HP])
        kcat = sb("kcat", [P, IT * H, HP])
        qt = sb("qt", [P, NP, BANK], F32R)
        kt = sb("kt", [P, NP, BANK], F32R)
        mx = sb("mx", [P, 2, 2, 4, IT])
        mt = sb("mt", [2 * 4 * IT, 2, P], F32R)
        junk = sb("junk", [P, 2, BANK])
        gate_dve = sb("gate_dve", [P, 6 * NP + 1])
        gate_pool = sb("gate_pool", [P, 3 * NP])
        probs = sb("probs", [P, 2, 5 * BANK])
        v_sb = sb("v_sb", [P, IT * H, VW])
        ao_t = sb("ao_t", [P, H // 4, BANK])
        rec = sb("rec", [P, 2, H])
        ao = sb("ao", [P, IT, D])
        aot_hi = sb("aot_hi", [P, BANK], F32R)
        aot_lo = sb("aot_lo", [P, BANK], F32R)

        ld = sem("ld")
        const = sem("const")
        link_dve = sem("link_dve")
        w_done = sem("w_done")
        xn_done = sem("xn_done")
        bout_added = sem("bout_added")
        x_added = sem("x_added")
        t_full = sem("t_full")
        t_half = sem("t_half")
        t_free = sem("t_free")
        m_full = [sem(f"m_full{i}") for i in range(2)]
        m_free = [sem(f"m_free{i}") for i in range(2)]
        s_full = sem("s_full")
        s_free = sem("s_free")
        masked = sem("masked")
        pv_done = sem("pv_done")
        pv_free = sem("pv_free")
        cats_done = sem("cats_done")
        raw_done = sem("raw_done")
        qk_in = sem("qk_in")
        lines_in = sem("lines_in")
        v_done = sem("v_done")
        mt_done = sem("mt_done")
        m_row = [sem(f"m_row{i}") for i in range(2)]

        S = [psum[:, 0:2, :], psum[:, 2:4, :]]
        M = [psum[:, 4, :], psum[:, 5, :]]
        T = psum[:, 6, :]
        PV = psum[:, 7, :]

        def heads(ap):
            return ap.rearrange("p (i h) k -> p i h k", h=H)

        def wait(eng, s, value):
            if not (isinstance(value, int) and value <= 0):
                eng.wait_ge(s, value)

        def pipeline(eng, body, counts):
            body(0, None, None)
            body(1, 0, None)
            with eng.Fori(0, NB - 2) as i:
                for c, k in counts:
                    c.enter(i, k)
                body(i + 2, i + 1, i)
                for c, k in counts:
                    c.leave(NB - 2, k)
            body(None, NB - 1, NB - 2)
            body(None, None, NB - 1)

        T_USES = 4 + 2 * NP
        T_FREES = 2 + 2 * NP
        M_WRITES = [2 + 2 + 1 + 3 * NP, 2 + 2 + 3 * NP]
        M_READS = [2 + 2 + 1 + 4 * NP, 2 + 2 + 4 * NP]
        CHAIN = IT + 5 + 10 + 2
        CONSTS = 11

        block = ctx.enter_context(nc.Block())

        @block.sync
        def _(sp):
            sp.wait_ge(const, 1)
            for dst, src in (
                (w_raw[:, 0:3 * D], dram["wqkv"]),
                (w_raw[:, 3 * D:3 * D + 4 * H], dram["w1p"]),
                (w_raw[:, 3 * D + 4 * H:], dram["w2p"]),
                (wo_raw[:], dram["wout"]),
                (bias[:, 0:3 * D], dram["bqkv"].partition_broadcast(P)),
                (bout[:], dram["bout"].partition_broadcast(P)),
                (pscale[:], dram["scale"].partition_broadcast(P)),
            ):
                sp.dma_start(dst, src).then_inc(ld, 16)

            def rows(hf, value):
                sp.wait_ge(mt_done, value)
                for hh in range(2):
                    sp.dma_start(qt[HP * hh + K - 1:HP * hh + K, 4 * hf:4 * hf + 4, :].bitcast(F32).rearrange("a b (t c) -> a (b t) c", c=P),
                                 mt[4 * IT * hh:4 * IT * (hh + 1), hf, :].bitcast(F32)).then_inc(m_row[hf], 16)

            rows(0, 1)
            with sp.Fori(0, NB - 1) as i:
                rows(1, i * 2 + 2)
                rows(0, i * 2 + 3)
            rows(1, 2 * NB)
            sp.wait_ge(m_row[0], 32 * NB)
            sp.wait_ge(m_row[1], 32 * NB)

        @block.gpsimd
        def _(pool):
            nc.gpsimd.memset(bias[:], 0.0).then_inc(const, 1)
            links = 1

            def link(ins):
                nonlocal links
                links += 1
                ins.then_inc(const, 1)
                pool.wait_ge(const, links)

            nc.gpsimd.memset(qcat[:], 0.0).then_inc(const, 1)
            nc.gpsimd.memset(mx[:], 0.0).then_inc(const, 1)
            links += 2
            link(nc.gpsimd.memset(kcat[:], 0.0))
            link(nc.gpsimd.memset(kcat[:, :, K - 1:K], -1.0))
            link(nc.gpsimd.memset(v_sb[:], 0.0))
            link(nc.gpsimd.memset(v_sb[:, :, DH:DH + 1], 1.0))
            link(nc.gpsimd.memset(causal[:], 0.0))
            link(nc.gpsimd.affine_select(out=causal[:, BANK - P:], in_=causal[:, BANK - P:], compare_op=ALU.is_ge,
                                         fill=-3.0e38, base=0, pattern=[[-1, P]], channel_multiplier=1))
            pool.wait_ge(ld, 16 * 7)
            link(nc.gpsimd.tensor_copy(line_scale[:], pscale[:].unsqueeze(2).to_broadcast([P, H, NC])))
            link(nc.gpsimd.tensor_scalar(line_scale[:, :, 1:5:3], line_scale[:, :, 1:5:3], -1.0, None, ALU.mult))
            assert links == CONSTS
            s_n = Count()

            def exponentiated():
                pool.wait_ge(s_free, s_n.step())
                i = (s_n.local - 1) % (3 * NP)
                nc.gpsimd.tensor_tensor(gate_pool[:, i:i + 1], ident[:, 0:1], ident[:, 0:1], ALU.add)

            def keep(view, blocks):
                return nc.gpsimd.affine_select(out=view, in_=view, compare_op=ALU.is_ge, fill=0.0, base=0,
                                               pattern=[[0, blocks]] * (blocks > 1) + [[1, P]], channel_multiplier=-1)

            def body(c, b, d):
                if c is not None:
                    pool.wait_ge(xn_done, c + 1)
                    xv = x_sb[:, bass.ds(c * IT, IT), :]
                    nc.gpsimd.tensor_tensor(xv, xv, bout[:].unsqueeze(1).to_broadcast([P, IT, D]),
                                            ALU.add).then_inc(bout_added, 1)
                if b is None:
                    return
                for p in range(NP):
                    pr = probs[:, p % 2, :]
                    for h in range(2):
                        exponentiated()
                        o = 2 * BANK * h
                        keep(pr[:, o:o + P], 1)
                        keep(pr[:, o + BANK:o + BANK + 2 * P].rearrange("p (a c) -> p a c", a=2), 2).then_inc(masked, 1)
                    exponentiated()
                    g = pr[:, 4 * BANK:].rearrange("p (a c) -> p a c", a=2)[:, :, 0:P]
                    keep(g, 2).then_inc(masked, 1)

            pipeline(pool, body, [(s_n, 3 * NP)])

        @block.scalar
        def _(act):
            t_n, s_n, g_n, pv_n = Count(), Count(), Count(), Count()

            def group(p, g, b):
                n = s_n.now()
                act.wait_ge(s_full, n + 1)
                if g == 0:
                    wait(act, pv_done, pv_n.now() - 1)
                    pv_n.step()
                src = S[(3 * p + g) % 2]
                dst = probs[:, p % 2, :]
                if g < 2:
                    out, in_ = dst[:, 2 * BANK * g:2 * BANK * (g + 1)], src.rearrange("p a c -> p (a c)")
                else:
                    out, in_ = dst[:, 4 * BANK:].rearrange("p (a c) -> p a c", a=2), src[:, :, 0:BANK // 2]
                nc.scalar.activation(out, in_, ACT.Exp).then_inc(s_free, 1)
                s_n.step()

            def take(dst, needed):
                act.wait_ge(t_full, t_n.step())
                wait(act, s_full, needed)
                nc.scalar.copy(dst, T).then_inc(t_free, 1)

            def high(dst):
                act.wait_ge(t_full, t_n.step())
                nc.scalar.copy(dst, T).then_inc(t_half, 1)

            def pv_out(g):
                act.wait_ge(pv_done, g_n.step(2))
                nc.scalar.copy(ao_t[:, g, :], PV).then_inc(pv_free, 1)

            def body(c, b, d):
                for p in range(NP):
                    if p == 1 and b is not None:
                        t_n.step()
                    if p == 7 and c is not None:
                        t_n.step()
                    if p == 1 and d is not None:
                        pv_out(3)
                    if b is not None and p in (3, 5, 7):
                        pv_out((p - 3) // 2)
                    pairs = (2 * (p - 4), 2 * (p - 4) + 1) if c is not None and p >= 4 else ()

                    def needed(a):
                        return 0 if b is None else first + 3 * a

                    if b is not None:
                        group(p, 0, b)
                    if pairs:
                        take(qt[:, pairs[0], :], needed(pairs[0]))
                    if p == 2 and d is not None:
                        high(aot_hi[:])
                    if p == 3 and c is not None:
                        act.wait_ge(lines_in, c + 1)
                        act.wait_ge(qk_in, c * 4 + 2)
                        for at in (0, 2 * C):
                            nc.scalar.copy(kcat[:, :, at:at + C].bitcast(F32R), kf[:]).then_inc(qk_in, 1)
                    if b is not None:
                        group(p, 1, b)
                    if pairs:
                        take(kt[:, pairs[0], :], needed(pairs[0]))
                    if b is not None:
                        group(p, 2, b)
                        if p == 0:
                            first = s_n.now()
                    if p == 0 and c is not None:
                        high(xt_hi[:])
                    if p == 1 and c is not None:
                        act.wait_ge(raw_done, c + 1)
                        nc.scalar.activation(heads(qf[:])[:, :, :, 0:DH],
                                             raw[:, :, 0:D].rearrange("p i (h k) -> p i h k", k=DH), ACT.Copy,
                                             scale=QSCALE).then_inc(qk_in, 1)
                        nc.scalar.copy(heads(kf[:])[:, :, :, 0:DH],
                                       raw[:, :, D:2 * D].rearrange("p i (h k) -> p i h k", k=DH)).then_inc(qk_in, 1)
                    if pairs:
                        take(qt[:, pairs[1], :], needed(pairs[1]))
                        take(kt[:, pairs[1], :], needed(pairs[1]))

            pipeline(act, body, [(t_n, T_USES), (s_n, 3 * NP), (g_n, NP), (pv_n, NP)])

        @block.vector
        def _(dve):
            chain = Count()

            def link(ins):
                ins.then_inc(link_dve, 1)
                dve.wait_ge(link_dve, chain.step())

            def rsqrt(r, v, t):
                I32 = mybir.dt.int32
                link(nc.vector.tensor_scalar(r.bitcast(I32), v.bitcast(I32), -0.5, RSQRT_MAGIC, ALU.mult, ALU.add))
                for _ in range(3):
                    link(nc.vector.scalar_tensor_tensor(t, r, -0.5, v, ALU.mult, ALU.mult))
                    link(nc.vector.tensor_tensor(t, t, r, ALU.mult))
                    link(nc.vector.scalar_tensor_tensor(r, t, 1.5, r, ALU.add, ALU.mult))

            for t in range(NT):
                last = nc.vector.bn_stats(stats[:, t, :], x_sb[:, t, :])
            link(last)
            for t in range(NT):
                last = nc.vector.bn_aggr(mv[:, t, :], stats[:, t, :])
            link(last)
            link(nc.vector.tensor_scalar(var[:], mv[:, :, 1], EPS, None, ALU.add))
            rsqrt(rstd[:], var[:], newton[:])
            dve.wait_ge(ld, 16 * 7)
            link(nc.vector.tensor_copy(w_hi[:], w_raw[:]))
            nc.vector.tensor_tensor(w_lo[:], w_raw[:], w_hi[:].bitcast(F32), ALU.subtract).then_inc(w_done, 1)
            link(nc.vector.tensor_copy(wo_hi[:], wo_raw[:]))
            nc.vector.tensor_tensor(wo_lo[:], wo_raw[:], wo_hi[:].bitcast(F32), ALU.subtract).then_inc(w_done, 1)

            dve.wait_ge(const, CONSTS)

            t_n, half_n, m_n, m_r = Count(), Count(), [Count(), Count()], [Count(), Count()]
            p1 = raw[:, :, 3 * D:3 * D + 4 * H].rearrange("p i (h k) -> p i h k", k=4)
            p2 = raw[:, :, 3 * D + 4 * H:].rearrange("p i (h k) -> p i h k", k=4)

            def filled(i):
                dve.wait_ge(m_full[i], m_n[i].step())

            def release(i, ins):
                m_r[i].step()
                return ins.then_inc(m_free[i], 1)

            def maxima_out(hf, c):
                dve.wait_ge(t_full, t_n.step())
                wait(dve, m_row[hf], c * 32)
                nc.vector.tensor_copy(mt[:, hf, :], T[0:2 * 4 * IT, 0:P]).then_inc(mt_done, 1)

            def low(dst, hi):
                t_n.step()
                dve.wait_ge(t_half, half_n.step())
                nc.vector.tensor_tensor(dst, T, hi.bitcast(F32), ALU.subtract).then_inc(t_free, 1)

            def normalise(c):
                for s in range(IT):
                    t = c * IT + s
                    last = nc.vector.tensor_scalar(
                        xn[:, P * s:P * (s + 1)], x_sb[:, bass.ds(t, 1), :].rearrange("p a d -> p (a d)"),
                        mv[:, bass.ds(t, 1), 0], rstd[:, bass.ds(t, 1)], ALU.subtract, ALU.mult)
                last.then_inc(xn_done, 1)

            def divide(it):
                i = it % 2
                filled(i)
                o = M[i].rearrange("p (h k) -> p h k", k=VW)
                link(nc.vector.reciprocal(rec[:, i, :], o[:, :, DH]))
                release(i, nc.vector.tensor_tensor(ao[:, it, :].rearrange("p (h k) -> p h k", k=DH), o[:, :, 0:DH],
                                                   rec[:, i, :].unsqueeze(2).to_broadcast([P, H, DH]), ALU.mult))

            def lines(c):
                for x, y, out in ((p1, p2, heads(la[:])), (p2, p1, heads(lb[:]))):
                    for i, o in ((0, 0), (1, 3), (2, 5)):
                        w = 3 - i
                        last = nc.vector.tensor_tensor(out[:, :, :, o:o + w], y[:, :, :, i + 1:4],
                                                       x[:, :, :, i:i + 1].to_broadcast([P, IT, H, w]), ALU.mult)
                link(last)
                link(nc.vector.tensor_tensor(la[:], la[:], lb[:], ALU.subtract))
                link(nc.vector.tensor_tensor(lb[:], la[:], la[:], ALU.mult))
                link(nc.vector.reduce_sum(ss[:], lb[:], AX_X))
                link(nc.vector.tensor_scalar(ss[:], ss[:], 1e-24, None, ALU.max))

            def operands(c):
                rsqrt(rn[:], ss[:], nw[:])
                shape = [P, IT * H, NC]
                link(nc.vector.tensor_tensor(kf[:, :, DH:C], la[:], rn[:].unsqueeze(2).to_broadcast(shape), ALU.mult))
                nc.vector.tensor_tensor(heads(qf[:])[:, :, :, DH:C], heads(kf[:])[:, :, :, DH:C][:, :, :, ::-1],
                                        line_scale[:].unsqueeze(1).to_broadcast([P, IT, H, NC]),
                                        ALU.mult).then_inc(lines_in, 1)
                dve.wait_ge(lines_in, c + 1)
                dve.wait_ge(qk_in, c * 4 + 2)
                link(nc.vector.tensor_copy(qcat[:, :, 0:2 * C].bitcast(F32R).rearrange("p a (t c) -> p a t c", c=C),
                                           qf[:].unsqueeze(2).to_broadcast([P, IT * H, 2, C])))
                nc.vector.tensor_tensor(qcat[:, :, 2 * C:3 * C].bitcast(F32R), qf[:], qcat[:, :, 0:C],
                                        ALU.subtract).then_inc(cats_done, 1)
                dve.wait_ge(qk_in, c * 4 + 3)
                nc.vector.tensor_tensor(kcat[:, :, C:2 * C].bitcast(F32R), kf[:], kcat[:, :, 0:C],
                                        ALU.subtract).then_inc(cats_done, 1)

            def row_max(a, hh, it):
                w = P * (it + 1)
                o = P if it == 1 else 0
                release(hh, nc.vector.tensor_tensor_reduce(
                    out=junk[:, hh, o:o + w], in0=M[hh][:, o:o + w], in1=causal[:, BANK - w:], scale=1.0, scalar=-3.0e38,
                    op0=ALU.add, op1=ALU.max, accum_out=mx[:, a // 4, hh, a % 4, it:it + 1]))

            def row_maxima(a):
                for k, its in enumerate(((0, 1), (2,), (3,))):
                    for hh in range(2):
                        filled(hh)
                        at = (a * 3 + k) * 2 + hh
                        nc.vector.memset(gate_dve[:, at:at + 1], 0.0)
                        for it in its:
                            row_max(a, hh, it)

            def copy_v(b):
                if not isinstance(b, int) or b > 0:
                    dve.wait_ge(pv_done, b * NP)
                nc.vector.tensor_copy(heads(v_sb[:])[:, :, :, 0:DH],
                                      raw[:, :, 2 * D:3 * D].rearrange("p i (h k) -> p i h k", k=DH)).then_inc(v_done, 1)
                dve.wait_ge(v_done, b + 1)

            def body(c, b, d):
                if b is not None:
                    row_maxima(NP - 1)
                if c is not None:
                    normalise(c)
                if c is not None:
                    low(xt_lo[:], xt_hi[:])
                if b is not None:
                    copy_v(b)
                if c is not None:
                    for it in range(IT):
                        filled(it % 2)
                        release(it % 2, nc.vector.tensor_tensor(raw[:, it, :], M[it % 2], bias[:], ALU.add))
                    for i in range(2):
                        dve.wait_ge(m_free[i], m_r[i].now())
                    nc.vector.memset(gate_dve[:, 6 * NP:], 0.0).then_inc(raw_done, 1)
                if b is not None:
                    maxima_out(1, b)
                if d is not None:
                    for it in range(IT):
                        divide(it)
                if c is not None:
                    lines(c)
                if c is not None:
                    operands(c)
                if d is not None:
                    low(aot_lo[:], aot_hi[:])
                if d is not None:
                    filled(0)
                    dve.wait_ge(bout_added, d + 1)
                    xv = x_sb[:, bass.ds(d * IT, IT), :]
                    release(0, nc.vector.tensor_tensor(xv, M[0].rearrange("p (a d) -> p a d", d=D), xv, ALU.add))
                if c is not None:
                    for a in range(NP - 1):
                        if a == 5:
                            t_n.step(12)
                            maxima_out(0, c)
                            t_n.step(4)
                        row_maxima(a)

            pipeline(dve, body, [(t_n, T_USES), (half_n, 2), (m_n[0], M_WRITES[0]), (m_n[1], M_WRITES[1]),
                                 (m_r[0], M_READS[0]), (m_r[1], M_READS[1]), (chain, CHAIN)])

        @block.tensor
        def _(pe):
            t_n, t_r, mt_n, s_n, pv_n, g_n = Count(), Count(), Count(), Count(), Count(), Count()
            m_r = [Count(), Count()]
            freed = [None]

            def product(out, a_hi, a_lo, b_hi, b_lo):
                nc.tensor.matmul(out, a_hi, b_hi, start=True, stop=False)
                nc.tensor.matmul(out, a_hi, b_lo, start=False, stop=False)
                return nc.tensor.matmul(out, a_lo, b_hi, start=False, stop=True)

            def transposes(pieces, maxima=False):
                pe.wait_ge(t_free, t_r.now()) if not (isinstance(t_r.now(), int) and t_r.now() == 0) else None
                wait(pe, mt_done, mt_n.now())
                for dst, src in pieces:
                    last = nc.tensor.transpose(dst, src, ident[:])
                last.then_inc(t_full, 1)
                (mt_n if maxima else t_r).step()

            def bank(i, reads):
                wait(pe, m_free[i], m_r[i].now())
                m_r[i].step(reads)

            def maxima(hf):
                for i in range(2):
                    wait(pe, m_free[i], m_r[i].now())
                transposes([(T[0:2 * 4 * IT, 0:P], mx[:, hf, :, :, :].rearrange("p a b c -> p (a b c)"))], maxima=True)

            def pair(cat, a):
                return [(T[:, P * it:P * (it + 1)],
                         cat[:, H * it + 2 * a:H * it + 2 * a + 2, :].rearrange("p a c -> p (a c)")) for it in range(IT)]

            def logits(p, g):
                n = s_n.step()
                wait(pe, s_free, n - 2)
                s = S[(3 * p + g) % 2]

                def one(hh, jt, out):
                    r = slice(HP * hh, HP * hh + K)
                    return nc.tensor.matmul(out, kt[r, p, P * jt:P * (jt + 1)], qt[r, p, P * jt:], start=True, stop=True)

                if g < 2:
                    one(g, 0, s[:, 0, :])
                    one(g, 3, s[:, 1, 0:P])
                    one(g, 1, s[:, 1, P:]).then_inc(s_full, 1)
                else:
                    one(0, 2, s[:, 0, 0:2 * P])
                    one(1, 2, s[:, 1, 0:2 * P]).then_inc(s_full, 1)

            def values(p, k):
                hh, jt = k // 4, k % 4
                h = 2 * p + hh
                out = PV[VW * (h % 4):VW * (h % 4 + 1), P * jt:]
                at = (2 * BANK * hh, 2 * BANK * hh + BANK + P, 4 * BANK + 2 * P * hh, 2 * BANK * hh + BANK)[jt]
                if k == 0:
                    pe.wait_ge(masked, pv_n.now() * 3 + 3)
                    if p % 2 == 0:
                        wait(pe, pv_free, g_n.now())
                        g_n.step()
                last = nc.tensor.matmul(out, v_sb[:, H * jt + h, :], probs[:, p % 2, at:at + BANK - P * jt],
                                        start=jt == 0, stop=jt == 3)
                if k == 7:
                    last.then_inc(pv_done, 1)
                    pv_n.step()

            def row_logits(a, part, hh):
                bank(hh, 2 if part == 0 else 1)
                r = slice(HP * hh, HP * hh + K)
                for it in (0, 1) if part == 0 else (part + 1,):
                    w = P * (it + 1)
                    o = P if it == 1 else 0
                    last = nc.tensor.matmul(M[hh][:, o:o + w], qt[r, a, P * it:P * (it + 1)], kt[r, a, 0:w],
                                            start=True, stop=True)
                last.then_inc(m_full[hh], 1)

            def project(c, it):
                bank(it % 2, 1)
                t = slice(P * it, P * (it + 1))
                product(M[it % 2], xt_hi[:, t], xt_lo[:, t], w_hi[:], w_lo[:]).then_inc(m_full[it % 2], 1)

            def divide_in(it):
                bank(it % 2, 1)
                for g in range(H // 4):
                    last = nc.tensor.transpose(M[it % 2][:, P * g:P * (g + 1)], ao_t[:, g, P * it:P * (it + 1)], ident[:])
                last.then_inc(m_full[it % 2], 1)

            def out_project():
                pe.wait_ge(w_done, 2)
                pe.wait_ge(t_free, t_r.now())
                bank(0, 1)
                for it in range(IT):
                    t = slice(P * it, P * (it + 1))
                    last = product(M[0][:, P * it:P * (it + 1)], aot_hi[:, t], aot_lo[:, t], wo_hi[:], wo_lo[:])
                last.then_inc(m_full[0], 1)

            def body(c, b, d):
                def lg(p, g):
                    if b is not None:
                        if g == 0 and p in (0, 4):
                            pe.wait_ge(m_row[p // 4], b * 32 + 32)
                        logits(p, g)

                def pv(p, *ks):
                    if (b if p else d) is not None:
                        for k in ks:
                            if p == 1 and k == 0:
                                pe.wait_ge(v_done, b + 1)
                            values((p - 1) % NP, k)

                lg(0, 0)
                if b is not None:
                    pe.wait_ge(t_free, t_r.now())
                for i in range(6):
                    if b is not None:
                        row_logits(NP - 1, i // 2, i % 2)
                    pv(0, i)
                    if i in (1, 3):
                        lg(0, (i + 1) // 2)
                if c is not None:
                    pe.wait_ge(xn_done, c + 1)
                    transposes([(T[:, P * s:P * (s + 1)], xn[:, P * s:P * (s + 1)]) for s in range(IT)])
                pv(0, 6, 7)
                lg(1, 0)
                if c is not None:
                    pe.wait_ge(w_done, 1)
                    pe.wait_ge(t_free, t_r.now())
                    project(c, 0)
                    project(c, 1)
                pv(1, 0)
                lg(1, 1)
                if c is not None:
                    project(c, 2)
                if b is not None:
                    maxima(1)
                if c is not None:
                    project(c, 3)
                pv(1, 1)
                if d is not None:
                    pe.wait_ge(pv_free, d * 4 + 4)
                    divide_in(0)
                pv(1, 2)
                if d is not None:
                    divide_in(1)
                lg(1, 2)
                pv(1, 3)
                if d is not None:
                    divide_in(2)
                pv(1, 4)
                if d is not None:
                    divide_in(3)
                pv(1, 5, 6, 7)
                lg(2, 0)
                pv(2, 0)
                if d is not None:
                    for i in range(2):
                        pe.wait_ge(m_free[i], m_r[i].now())
                    transposes([(T[:, P * it:P * (it + 1)], ao[:, it, :]) for it in range(IT)])
                lg(2, 1)
                pv(2, 1, 2, 3)
                lg(2, 2)
                pv(2, 4, 5, 6, 7)
                lg(3, 0)
                pv(3, 0)
                lg(3, 1)
                pv(3, 1, 2, 3)
                lg(3, 2)
                pv(3, 4, 5, 6, 7)
                for p in range(4, NP):
                    a = 2 * (p - 4)
                    if c is not None:
                        if p == 4:
                            pe.wait_ge(cats_done, c * 2 + 2)
                            pe.wait_ge(qk_in, c * 4 + 4)
                        if p == 7:
                            maxima(0)

                    def turn(cat, n):
                        if c is not None:
                            transposes(pair(cat, n))

                    def rl(n, part, hh):
                        if c is not None and n >= 0:
                            row_logits(n, part, hh)

                    lg(p, 0)
                    if p == 4 and d is not None:
                        out_project()
                    turn(qcat, a)
                    rl(a - 1, 0, 0)
                    pv(p, 0)
                    rl(a - 1, 0, 1)
                    lg(p, 1)
                    turn(kcat, a)
                    pv(p, 1)
                    rl(a - 1, 1, 0)
                    rl(a - 1, 1, 1)
                    pv(p, 2, 3)
                    rl(a - 1, 2, 0)
                    lg(p, 2)
                    rl(a - 1, 2, 1)
                    turn(qcat, a + 1)
                    pv(p, 4)
                    rl(a, 0, 0)
                    rl(a, 0, 1)
                    turn(kcat, a + 1)
                    pv(p, 5)
                    rl(a, 1, 0)
                    rl(a, 1, 1)
                    pv(p, 6)
                    rl(a, 2, 0)
                    pv(p, 7)
                    rl(a, 2, 1)

            pipeline(pe, body, [(t_r, T_FREES), (mt_n, 2), (s_n, 3 * NP), (pv_n, NP), (g_n, NP // 2),
                                (m_r[0], M_READS[0]), (m_r[1], M_READS[1])])


def ffn_phase(nc, tag, psum, x_sb, ident, dram, x_in, y_out):
    NT = x_sb.shape[1]
    D = x_sb.shape[2]
    TOK = NT * P
    NE, _, F = dram["w_gate"].shape
    FC = F // P
    TT = TOK // BANK
    SUB = BANK // P
    NR = 2 * NE
    WCOLS = 3 * F
    CHUNK = WCOLS // TT
    HALF = TOK // 2
    assert D == P and FC == 4 and NE % 2 == 0 and WCOLS % TT == 0 and NT * NR == BANK

    with ExitStack() as ctx:
        def sb(name, shape, dt=F32):
            return ctx.enter_context(nc.sbuf_tensor(f"{name}_{tag}", shape, dt))

        def sem(name):
            return ctx.enter_context(nc.semaphore(f"{name}_{tag}"))

        xt_hi = sb("xt_hi", [P, TOK], F32R)
        xt_lo = sb("xt_lo", [P, TOK], F32R)
        f_acc = sb("f_acc", [P, TOK])
        w_raw = sb("w_raw", [P, 2, WCOLS])
        w_hi = sb("w_hi", [P, 2, WCOLS], F32R)
        w_lo = sb("w_lo", [P, 2, WCOLS], F32R)
        wr_raw = sb("wr_raw", [P, P])
        wr_hi = sb("wr_hi", [P, P], F32R)
        wr_lo = sb("wr_lo", [P, P], F32R)
        xn = sb("xn", [P, 2, BANK])
        stats = sb("stats", [P, NT, 6])
        mv = sb("mv", [P, NT, 2])
        rstd = sb("rstd", [P, NT])
        var = sb("var", [P, NT])
        newton = sb("newton", [P, NT])
        logit_t = sb("logit_t", [NR, TOK])
        probs = sb("probs", [P, NT, 2, NE])
        red = sb("red", [P, NT * 2])
        cw = sb("cw", [P, 2, NE, NT // 2])
        cws = sb("cws", [P, NT])
        cw_rows = sb("cw_rows", [P, 2, P])
        cwb = sb("cwb", [P, 2, TOK])
        s_buf = sb("s_buf", [P, 2, BANK])
        h_buf = sb("h_buf", [P, 2, BANK])
        h_hi = sb("h_hi", [P, FC, BANK], F32R)
        h_lo = sb("h_lo", [P, FC, BANK], F32R)
        o_tmp = sb("o_tmp", [P, BANK])

        x_ld = [sem(f"x_ld{i}") for i in range(TT)]
        w_ld = [sem(f"w_ld{i}") for i in range(2)]
        cwb_ld = [sem(f"cwb_ld{i}") for i in range(2)]
        wr_ld = sem("wr_ld")
        wr_zero = sem("wr_zero")
        f_zero = sem("f_zero")
        dve_link = sem("dve_link")
        var_done = sem("var_done")
        std_done = sem("std_done")
        xn_done = sem("xn_done")
        xt_tr = sem("xt_tr")
        xt_hi_done = sem("xt_hi_done")
        xt_lo_done = sem("xt_lo_done")
        w0_hi = sem("w0_hi")
        w0_done = sem("w0_done")
        wr_done = sem("wr_done")
        logit_mm = sem("logit_mm")
        logit_cp = sem("logit_cp")
        logit_tr = sem("logit_tr")
        shifted = sem("shifted")
        exp_done = sem("exp_done")
        cw_done = sem("cw_done")
        cw_tr = sem("cw_tr")
        cw_cp = sem("cw_cp")
        cw_st = sem("cw_st")
        gu_done = sem("gu_done")
        silu_done = sem("silu_done")
        h_done = sem("h_done")
        hi_done = sem("hi_done")
        lo_done = sem("lo_done")
        down_done = sem("down_done")
        o_read = sem("o_read")
        o_added = sem("o_added")
        w_chunk = sem("w_chunk")
        w_chunk_hi = sem("w_chunk_hi")
        f_tr = sem("f_tr")
        x_new = sem("x_new")
        y_st = sem("y_st")

        G = [psum[:, 0, :], psum[:, 1, :]]
        U = [psum[:, 2, :], psum[:, 3, :]]
        def O(t):
            return psum[:, bass.ds(4 + t % 2, 1), :].rearrange("p a c -> p (a c)")

        XT = [psum[:, 6, :], psum[:, 7, :]]
        LT = [psum[:, 4, :], psum[:, 5, :]]
        LG = psum[:, 6, :]
        CT = psum[:, 7, 0:2 * P]
        FT = [psum[:, 6, :], psum[:, 7, :]]

        def wait(eng, s, value):
            if not (isinstance(value, int) and value <= 0):
                eng.wait_ge(s, value)

        def over_tiles(eng, tile):
            tile(0, 0, 0, 0, None)
            with eng.Fori(1, TT) as t:
                tile(t, 0, t, 0, 0)
            with eng.Fori(0, NE // 2 - 1) as m:
                for d in (1, 2):
                    e = 2 * m + d
                    n0 = m * (2 * TT) + TT * d
                    tile(n0, e, 0, d % 2, 0 if d == 1 else 2)
                    with eng.Fori(1, TT) as t:
                        tile(n0 + t, e, t, d % 2, 1)
            e = NE - 1
            tile(TT * e, e, 0, 1, 2)
            with eng.Fori(1, TT) as t:
                tile(t + TT * e, e, t, 1, 1)

        block = ctx.enter_context(nc.Block())

        @block.sync
        def _(sp):
            if x_in is not None:
                x_view = x_in.rearrange("(t p) d -> p t d", p=P)
                for j in range(TT):
                    sp.dma_start(x_sb[:, SUB * j:SUB * (j + 1), :],
                                 x_view[:, SUB * j:SUB * (j + 1), :]).then_inc(x_ld[j], 16)

            def load_expert(e, par):
                sp.dma_start(w_raw[:, par, 0:F],
                             dram["w_gate"][bass.ds(e, 1)].rearrange("a k f -> k (a f)")).then_inc(w_ld[par], 16)
                sp.dma_start(w_raw[:, par, F:2 * F],
                             dram["w_up"][bass.ds(e, 1)].rearrange("a k f -> k (a f)")).then_inc(w_ld[par], 16)
                sp.dma_start(w_raw[:, par, 2 * F:].rearrange("p (c h) -> p c h", c=FC),
                             dram["w_down"][bass.ds(e, 1)].rearrange("a (c p) h -> p (a c) h",
                                                                     p=P)).then_inc(w_ld[par], 16)

            def load_cw(e, par):
                for c in range(2):
                    sp.dma_start(cwb[:, par, HALF * c:HALF * (c + 1)],
                                 dram["cw_rows_" + tag][c, bass.ds(e, 1), :].partition_broadcast(P)
                                 ).then_inc(cwb_ld[par], 16)

            sp.wait_ge(wr_zero, 1)
            sp.dma_start(wr_raw[:, 0:NE], dram["w_router"]).then_inc(wr_ld, 16)
            sp.dma_start(wr_raw[:, NE:NR], dram["w_gating"]).then_inc(wr_ld, 16)
            load_expert(0, 0)
            load_expert(1, 1)
            sp.wait_ge(cw_cp, 1)
            for c in range(2):
                sp.dma_start(dram["cw_rows_" + tag][c].rearrange("e (t p) -> (e t) p", p=P),
                             cw_rows[:, c, :]).then_inc(cw_st, 16)
            sp.wait_ge(cw_st, 32)
            load_cw(0, 0)
            load_cw(1, 1)
            sp.wait_ge(w0_done, 1)
            load_expert(2, 0)
            sp.wait_ge(o_read, TT + 1)
            load_cw(2, 0)
            with sp.Fori(0, (NE - 4) // 2) as m:
                for d in (3, 4):
                    e = 2 * m + d
                    sp.wait_ge(w_chunk, m * (2 * TT) + TT * (d - 2))
                    load_expert(e, d % 2)
                    sp.wait_ge(o_read, m * (2 * TT) + (TT * (d - 1) + 1))
                    load_cw(e, d % 2)
            e = NE - 1
            sp.wait_ge(w_chunk, TT * (e - 2))
            load_expert(e, 1)
            sp.wait_ge(o_read, TT * (e - 1) + 1)
            load_cw(e, 1)
            if y_out is not None:
                y_view = y_out.rearrange("(t p) d -> p t d", p=P)
                for j in range(TT):
                    sp.wait_ge(x_new, j + 1)
                    sp.dma_start(y_view[:, SUB * j:SUB * (j + 1), :],
                                 x_sb[:, SUB * j:SUB * (j + 1), :]).then_inc(y_st, 16)
                sp.wait_ge(y_st, 16 * TT)

        @block.gpsimd
        def _(pool):
            nc.gpsimd.memset(wr_raw[:], 0.0).then_inc(wr_zero, 1)
            nc.gpsimd.memset(f_acc[:], 0.0).then_inc(f_zero, 1)

            def low_part(q, f):
                pool.wait_ge(hi_done, q + 1)
                nc.gpsimd.tensor_tensor(h_lo[:, f, :], h_buf[:, f % 2, :], h_hi[:, f, :].bitcast(F32),
                                        ALU.subtract).then_inc(lo_done, 1)

            with pool.Fori(0, TT * NE) as n:
                for f in range(FC):
                    low_part(n * FC + f, f)

        @block.scalar
        def _(act):
            act.wait_ge(w_ld[0], 48)
            nc.scalar.copy(w_hi[:, 0, :], w_raw[:, 0, :]).then_inc(w0_hi, 1)
            act.wait_ge(var_done, 1)
            nc.scalar.activation(rstd[:], var[:], ACT.Ln).then_inc(std_done, 1)
            act.wait_ge(std_done, 1)
            nc.scalar.activation(rstd[:], rstd[:], ACT.Exp, scale=-0.5).then_inc(std_done, 1)
            with act.Fori(0, TT // 2) as i:
                for b in range(2):
                    j = i * 2 + b
                    act.wait_ge(xt_tr, j + 1)
                    nc.scalar.copy(xt_hi[:, bass.ts(j, BANK)], XT[b]).then_inc(xt_hi_done, 1)
            with act.Fori(0, TT // 2) as i:
                for b in range(2):
                    j = i * 2 + b
                    act.wait_ge(logit_mm, j + 1)
                    nc.scalar.copy(logit_t[:, bass.ts(j, BANK)], LT[b][0:NR, :]).then_inc(logit_cp, 1)
            act.wait_ge(shifted, 1)
            nc.scalar.activation(probs[:, :, 0, :], probs[:, :, 0, :], ACT.Exp).then_inc(exp_done, 1)
            nc.scalar.activation(probs[:, :, 1, :], probs[:, :, 1, :], ACT.Exp, scale=10.0).then_inc(exp_done, 1)

            def silu(q, f):
                act.wait_ge(gu_done, q + 1)
                wait(act, h_done, q - 1)
                nc.scalar.activation(s_buf[:, f % 2, :], G[f % 2], ACT.Silu).then_inc(silu_done, 1)

            def high_part(q, f):
                act.wait_ge(h_done, q + 1)
                wait(act, down_done, q - (FC - 1))
                nc.scalar.copy(h_hi[:, f, :], h_buf[:, f % 2, :]).then_inc(hi_done, 1)

            def tile(n, e, t, par, prev):
                for f in range(FC):
                    q = n * FC + f
                    silu(q, f)
                    high_part(q, f)

            over_tiles(act, tile)

        @block.vector
        def _(dve):
            links = [0]

            def link(ins):
                links[0] += 1
                ins.then_inc(dve_link, 1)
                dve.wait_ge(dve_link, links[0])

            nc.vector.engine_nop().then_inc(o_read, 1)
            nc.vector.engine_nop().then_inc(o_added, 1)
            for t in range(NT):
                if x_in is not None and t % SUB == 0:
                    dve.wait_ge(x_ld[t // SUB], 16)
                last = nc.vector.bn_stats(stats[:, t, :], x_sb[:, t, :])
            link(last)
            for t in range(NT):
                last = nc.vector.bn_aggr(mv[:, t, :], stats[:, t, :])
            link(last)
            nc.vector.tensor_scalar(var[:], mv[:, :, 1], EPS, None, ALU.add).then_inc(var_done, 1)
            dve.wait_ge(w0_hi, 1)
            nc.vector.tensor_tensor(w_lo[:, 0, :], w_raw[:, 0, :], w_hi[:, 0, :].bitcast(F32),
                                    ALU.subtract).then_inc(w0_done, 1)
            dve.wait_ge(wr_ld, 32)
            link(nc.vector.tensor_copy(wr_hi[:], wr_raw[:]))
            nc.vector.tensor_tensor(wr_lo[:], wr_raw[:], wr_hi[:].bitcast(F32), ALU.subtract).then_inc(wr_done, 1)
            dve.wait_ge(std_done, 2)
            link(nc.vector.tensor_tensor(newton[:], rstd[:], rstd[:], ALU.mult))
            link(nc.vector.tensor_tensor(newton[:], newton[:], var[:], ALU.mult))
            link(nc.vector.tensor_scalar(newton[:], newton[:], -0.5, 1.5, ALU.mult, ALU.add))
            link(nc.vector.tensor_tensor(rstd[:], rstd[:], newton[:], ALU.mult))

            def normalise(j, b):
                wait(dve, xt_tr, j - 1)
                for s in range(SUB):
                    t = j * SUB + s
                    last = nc.vector.tensor_scalar(xn[:, b, P * s:P * (s + 1)], x_sb[:, bass.ds(t, 1), :].rearrange("p a d -> p (a d)"),
                                                   mv[:, bass.ds(t, 1), 0], rstd[:, bass.ds(t, 1)],
                                                   ALU.subtract, ALU.mult)
                last.then_inc(xn_done, 1)

            def low_xt(j, b):
                dve.wait_ge(xt_hi_done, j + 1)
                nc.vector.tensor_tensor(xt_lo[:, bass.ts(j, BANK)], XT[b], xt_hi[:, bass.ts(j, BANK)].bitcast(F32),
                                        ALU.subtract).then_inc(xt_lo_done, 1)

            normalise(0, 0)
            normalise(1, 1)
            with dve.Fori(0, TT // 2 - 1) as i:
                for b in range(2):
                    low_xt(i * 2 + b, b)
                    normalise(i * 2 + b + 2, b)
            low_xt(TT - 2, 0)
            low_xt(TT - 1, 1)

            dve.wait_ge(logit_tr, 1)
            lg = LG.rearrange("p (a e) -> p a e", e=NE)
            pr = probs[:].rearrange("p t s e -> p (t s) e")
            wide = [P, NT * 2, NE]
            link(nc.vector.reduce_max(red[:], lg, AX_X))
            nc.vector.tensor_tensor(pr, lg, red[:].unsqueeze(2).to_broadcast(wide), ALU.subtract).then_inc(shifted, 1)
            dve.wait_ge(exp_done, 2)
            link(nc.vector.reduce_sum(red[:], pr, AX_X))
            link(nc.vector.reciprocal(red[:], red[:]))
            link(nc.vector.tensor_tensor(pr, pr, red[:].unsqueeze(2).to_broadcast(wide), ALU.mult))
            link(nc.vector.tensor_tensor(probs[:, :, 0, :], probs[:, :, 0, :], probs[:, :, 1, :], ALU.mult))
            link(nc.vector.reduce_sum(cws[:], probs[:, :, 0, :], AX_X))
            link(nc.vector.tensor_scalar(cws[:], cws[:], 1e-9, None, ALU.add))
            link(nc.vector.reciprocal(cws[:], cws[:]))
            for c in range(2):
                last = nc.vector.tensor_tensor(
                    cw[:, c, :, :].rearrange("p e t -> p t e"), probs[:, NT // 2 * c:NT // 2 * (c + 1), 0, :],
                    cws[:, NT // 2 * c:NT // 2 * (c + 1)].unsqueeze(2).to_broadcast([P, NT // 2, NE]), ALU.mult)
            last.then_inc(cw_done, 1)

            def multiply(q, f):
                dve.wait_ge(silu_done, q + 1)
                wait(dve, lo_done, q - 1)
                nc.vector.tensor_tensor(h_buf[:, f % 2, :], U[f % 2], s_buf[:, f % 2, :],
                                        ALU.mult).then_inc(h_done, 1)

            def weigh(n, t, par, e):
                dve.wait_ge(cwb_ld[par], 32 * (e // 2 + 1) if isinstance(e, int) else e * 16 + (32 - 16 * par))
                dve.wait_ge(down_done, (n + 1) * FC)
                dve.wait_ge(o_added, n + 1)
                nc.vector.tensor_tensor(o_tmp[:], O(t), cwb[:, par, bass.ts(t, BANK)], ALU.mult).then_inc(o_read, 1)

            def add(n, t):
                dve.wait_ge(o_read, n + 2)
                nc.vector.tensor_tensor(f_acc[:, bass.ts(t, BANK)], f_acc[:, bass.ts(t, BANK)], o_tmp[:],
                                        ALU.add).then_inc(o_added, 1)

            def tile(n, e, t, par, prev):
                split = not (isinstance(e, int) and e == NE - 1)
                new = isinstance(t, int)
                pe, pt, ppar = (e - 1, TT - 1, 1 - par) if new else (e, t - 1, par)
                multiply(n * FC, 0)
                multiply(n * FC + 1, 1)
                if prev is not None:
                    weigh(n - 1, pt, ppar, pe)
                multiply(n * FC + 2, 2)
                if prev is not None:
                    add(n - 1, pt)
                cols = bass.ts(t, CHUNK)
                if split:
                    dve.wait_ge(w_ld[1 - par], 48 * ((e + 1) // 2 + 1) if isinstance(e, int) else e * 24 + (72 - 24 * (1 - par)))
                    nc.vector.tensor_copy(w_hi[:, 1 - par, cols], w_raw[:, 1 - par, cols]).then_inc(w_chunk_hi, 1)
                multiply(n * FC + 3, 3)
                if split:
                    dve.wait_ge(w_chunk_hi, n + 1)
                    nc.vector.tensor_tensor(w_lo[:, 1 - par, cols], w_raw[:, 1 - par, cols],
                                            w_hi[:, 1 - par, cols].bitcast(F32), ALU.subtract).then_inc(w_chunk, 1)
                if isinstance(n, int) and n == 0:
                    dve.wait_ge(cw_tr, 1)
                    nc.vector.tensor_copy(cw_rows[:].rearrange("p c q -> p (c q)"), CT).then_inc(cw_cp, 1)

            dve.wait_ge(f_zero, 1)
            over_tiles(dve, tile)
            last_n = TT * NE - 1
            weigh(last_n, TT - 1, 1, NE - 1)
            add(last_n, TT - 1)

            for j in range(TT):
                dve.wait_ge(f_tr, j + 1)
                xv = x_sb[:, SUB * j:SUB * (j + 1), :].rearrange("p a d -> p (a d)")
                nc.vector.scalar_tensor_tensor(xv, FT[j % 2], 0.5, xv, ALU.mult, ALU.add).then_inc(x_new, 1)

        @block.tensor
        def _(pe):
            def product(out, a_hi, a_lo, b_hi, b_lo, start, stop):
                nc.tensor.matmul(out, a_hi, b_hi, start=start, stop=False)
                nc.tensor.matmul(out, a_hi, b_lo, start=False, stop=False)
                return nc.tensor.matmul(out, a_lo, b_hi, start=False, stop=stop)

            with pe.Fori(0, TT // 2) as i:
                for b in range(2):
                    j = i * 2 + b
                    pe.wait_ge(xn_done, j + 1)
                    for s in range(SUB):
                        last = nc.tensor.transpose(XT[b][:, P * s:P * (s + 1)], xn[:, b, P * s:P * (s + 1)], ident[:])
                    last.then_inc(xt_tr, 1)
            pe.wait_ge(wr_done, 1)

            def router(j, b):
                pe.wait_ge(xt_lo_done, j + 1)
                wait(pe, logit_cp, j - 1)
                cols = bass.ts(j, BANK)
                product(LT[b], wr_hi[:], wr_lo[:], xt_hi[:, cols], xt_lo[:, cols], True, True).then_inc(logit_mm, 1)

            router(0, 0)
            router(1, 1)
            with pe.Fori(1, TT // 2) as i:
                for b in range(2):
                    router(i * 2 + b, b)
            pe.wait_ge(logit_cp, TT)
            for t in range(NT):
                last = nc.tensor.transpose(LG[:, NR * t:NR * (t + 1)], logit_t[:, P * t:P * (t + 1)], ident[0:NR, 0:NR])
            last.then_inc(logit_tr, 1)
            pe.wait_ge(w0_done, 1)

            def gate_up(q, f, t, par):
                wait(pe, h_done, q - 1)
                cols = bass.ts(t, BANK)
                for dst, at in ((G[f % 2], f * P), (U[f % 2], F + f * P)):
                    w = slice(at, at + P)
                    last = product(dst, w_hi[:, par, w], w_lo[:, par, w], xt_hi[:, cols], xt_lo[:, cols], True, True)
                last.then_inc(gu_done, 1)

            def down(q, f, par, n, t):
                pe.wait_ge(lo_done, q + 1)
                if f == 0:
                    wait(pe, o_read, n)
                w = slice(2 * F + f * P, 2 * F + (f + 1) * P)
                product(O(t), w_hi[:, par, w], w_lo[:, par, w], h_hi[:, f, :], h_lo[:, f, :],
                        f == 0, f == FC - 1).then_inc(down_done, 1)

            def tile(n, e, t, par, prev):
                new = isinstance(t, int)
                if new and prev is not None:
                    pe.wait_ge(w_chunk, n)
                ppar = 1 - par if new else par
                for f in range(FC):
                    q = n * FC + f
                    gate_up(q, f, t, par)
                    if f >= 2:
                        down(q - 2, f - 2, par, n, t)
                    elif prev is not None:
                        down(q - 2, f + 2, ppar, n - 1, TT - 1 if new else t - 1)
                if isinstance(n, int) and n == 0:
                    pe.wait_ge(cw_done, 1)
                    for c in range(2):
                        last = nc.tensor.transpose(CT[:, P * c:P * (c + 1)], cw[:, c, :, :].rearrange("p e t -> p (e t)"), ident[:])
                    last.then_inc(cw_tr, 1)

            over_tiles(pe, tile)
            last_q = TT * NE * FC
            down(last_q - 2, 2, 1, TT * NE - 1, TT - 1)
            down(last_q - 1, 3, 1, TT * NE - 1, TT - 1)
            pe.wait_ge(o_added, TT * NE + 1)
            for j in range(TT):
                if j >= 2:
                    pe.wait_ge(x_new, j - 1)
                for s in range(SUB):
                    t = j * SUB + s
                    last = nc.tensor.transpose(FT[j % 2][:, P * s:P * (s + 1)], f_acc[:, P * t:P * (t + 1)], ident[:])
                last.then_inc(f_tr, 1)


def macaron_block(nc, x, wqkv, bqkv, w1p, w2p, scale, wout, bout, w_router, w_gating, w_gate, w_up, w_down, out):
    D = x.shape[2]
    tokens = x.shape[0] * x.shape[1]
    NE = w_gate.shape[0]
    assert x.shape[1] == BANK, "a block of 512 columns is a sequence of the attention"
    x_rows, out_rows = (a.rearrange("b t d -> (b t) d") for a in (x, out))
    ffn = dict(w_router=w_router, w_gating=w_gating, w_gate=w_gate, w_up=w_up, w_down=w_down)
    for tag in ("f1", "f2"):
        ffn["cw_rows_" + tag] = nc.dram_tensor("cw_dram_" + tag, (2, NE, tokens // 2), F32, kind="Internal").ap()
    with ExitStack() as ctx:
        psum = ctx.enter_context(nc.psum_tensor("psum", [P, 8, BANK], F32))
        x_sb = ctx.enter_context(nc.sbuf_tensor("x_sb", [P, tokens // P, D], F32))
        ident = ctx.enter_context(nc.sbuf_tensor("ident", [P, P], F32))
        ident_zero = ctx.enter_context(nc.semaphore("ident_zero"))
        with nc.Block() as block:
            @block.gpsimd
            def _(pool):
                nc.gpsimd.memset(ident[:], 0.0).then_inc(ident_zero, 1)
                pool.wait_ge(ident_zero, 1)
                nc.gpsimd.affine_select(out=ident[:], in_=ident[:], compare_op=ALU.not_equal, fill=1.0, base=0,
                                        pattern=[[-1, P]], channel_multiplier=1).then_inc(ident_zero, 1)
                pool.wait_ge(ident_zero, 2)
        ffn_phase(nc, "f1", psum, x_sb, ident, ffn, x_rows, None)
        attention_phase(nc, psum, x_sb, ident, dict(wqkv=wqkv, bqkv=bqkv, w1p=w1p, w2p=w2p, scale=scale,
                                                    wout=wout, bout=bout))
        ffn_phase(nc, "f2", psum, x_sb, ident, ffn, None, out_rows)


_INS = ["L0_attn_x", "L0_attn_Wqkv", "L0_attn_bqkv", "L0_attn_W1p", "L0_attn_W2p", "L0_attn_plucker_scale",
        "L0_attn_Wout", "L0_attn_bout", "L0_ffn_w_router", "L0_ffn_w_gating", "L0_ffn_w_gate", "L0_ffn_w_up",
        "L0_ffn_w_down"]


def kernel(**inputs):
    import numpy as _np
    import concourse.bacc as _bacc
    from concourse import mybir as _mybir
    from concourse.bass_utils import run_bass_kernel_spmd as _run

    nc = _bacc.Bacc("TRN2", target_bir_lowering=False, num_devices=1)
    arrays, args = {}, []
    for name in _INS:
        a = _np.ascontiguousarray(inputs[name])
        arrays[f"in_{name}_dram"] = a
        args.append(nc.dram_tensor(f"in_{name}_dram", a.shape, _mybir.dt.from_np(a.dtype), kind="ExternalInput").ap())
    out = nc.dram_tensor("out_0_dram", inputs["L0_attn_x"].shape, _mybir.dt.float32, kind="ExternalOutput").ap()
    macaron_block(nc, *args, out)
    r = _run(nc, [arrays], core_ids=[0])
    return r.results[0]["out_0_dram"]
```

```python
from collections import namedtuple
from contextlib import ExitStack

import concourse.bass as bass
from concourse import mybir

F32 = mybir.dt.float32
F32R = mybir.dt.float32r
I32 = mybir.dt.int32
ALU = mybir.AluOpType
ACT = mybir.ActivationFunctionType
AX_X = mybir.AxisListType.X

P = 128
BANK = 512
EPS = 1e-5
RSQRT_MAGIC = float(0x5F3759DF)

Norm = namedtuple("Norm", "stats mv var rstd scratch")


def rsqrt(nc, link, r, v, t):
    link(nc.vector.tensor_scalar(r.bitcast(I32), v.bitcast(I32), -0.5, RSQRT_MAGIC, ALU.mult, ALU.add))
    for _ in range(3):
        link(nc.vector.scalar_tensor_tensor(t, r, -0.5, v, ALU.mult, ALU.mult))
        link(nc.vector.tensor_tensor(t, t, r, ALU.mult))
        link(nc.vector.scalar_tensor_tensor(r, t, 1.5, r, ALU.add, ALU.mult))


def norm_factors(nc, link, norm):
    for t in range(norm.stats.shape[1]):
        last = nc.vector.bn_aggr(norm.mv[:, t, :], norm.stats[:, t, :])
    link(last)
    link(nc.vector.tensor_scalar(norm.var[:], norm.mv[:, :, 1], EPS, None, ALU.add))
    rsqrt(nc, link, norm.rstd[:], norm.var[:], norm.scratch[:])


class Count:

    def __init__(self):
        self.base, self.local = 0, 0

    def now(self):
        return self.base + self.local

    def step(self, k=1):
        self.local += k
        return self.now()

    def enter(self, i, per_round):
        self.outer = self.base + self.local
        self.base, self.local = self.outer + i * per_round, 0

    def leave(self, rounds, per_round):
        assert self.local == per_round, (self.local, per_round)
        self.base, self.local = self.outer + rounds * per_round, 0


def attention_phase(nc, psum, x_sb, ident, norm, dram):
    NT, D = x_sb.shape[1:]
    H = dram["scale"].shape[0]
    DH = D // H
    NC = 6
    C = DH + NC
    K = 3 * C + 1
    HP = 64
    NP = H // 2
    IT = BANK // P
    NB = NT // IT
    PB = 4
    VW = 32
    assert DH == 8 and NP == 8 and K <= HP and NB >= 3
    QSCALE = float(DH) ** -0.5

    with ExitStack() as ctx:
        def sb(name, shape, dt=F32):
            return ctx.enter_context(nc.sbuf_tensor("a_" + name, shape, dt))

        def sem(name):
            return ctx.enter_context(nc.semaphore("a_" + name))

        w_raw = sb("w_raw", [P, BANK])
        w_hi = sb("w_hi", [P, BANK], F32R)
        w_lo = sb("w_lo", [P, BANK], F32R)
        wo_raw = sb("wo_raw", [P, D])
        wo_hi = sb("wo_hi", [P, D], F32R)
        wo_lo = sb("wo_lo", [P, D], F32R)
        bias = sb("bias", [P, BANK])
        bout = sb("bout", [P, D])
        pscale = sb("pscale", [P, H])
        line_scale = sb("line_scale", [P, H, NC])
        causal = sb("causal", [P, BANK])
        xn = sb("xn", [P, BANK])
        xt_hi = sb("xt_hi", [P, BANK], F32R)
        xt_lo = sb("xt_lo", [P, BANK], F32R)
        raw = sb("raw", [P, IT, BANK])
        la = sb("la", [P, IT * H, NC])
        lb = sb("lb", [P, IT * H, NC])
        ss = sb("ss", [P, IT * H])
        rn = sb("rn", [P, IT * H])
        nw = sb("nw", [P, IT * H])
        qf = sb("qf", [P, IT * H, C])
        kf = sb("kf", [P, IT * H, C])
        qcat = sb("qcat", [P, IT * H, HP])
        kcat = sb("kcat", [P, IT * H, HP])
        qt = sb("qt", [P, NP, BANK], F32R)
        kt = [sb(f"kt{hh}", [P, NP, BANK], F32R) for hh in range(2)]
        mx = sb("mx", [P, 2, 2, 4, IT])
        mt = sb("mt", [2 * 4 * IT, 2, P], F32R)
        junk = sb("junk", [P, 2, BANK])
        gate_dve = sb("gate_dve", [P, 6 * NP + 2])
        gate_pool = sb("gate_pool", [P, 3 * NP + 1])
        probs = sb("probs", [P, PB, 5 * BANK])
        v_hold = sb("v_hold", [P, IT, D])
        v_sb = sb("v_sb", [P, IT * H, VW])
        ao_t = sb("ao_t", [P, H // 4, BANK])
        rec = sb("rec", [P, 2, H])
        ao = sb("ao", [P, IT, D])
        aot_hi = sb("aot_hi", [P, BANK], F32R)
        aot_lo = sb("aot_lo", [P, BANK], F32R)

        ld = sem("ld")
        const = sem("const")
        link_dve = sem("link_dve")
        w_done = sem("w_done")
        xn_done = sem("xn_done")
        bout_added = sem("bout_added")
        t_full = sem("t_full")
        t_half = sem("t_half")
        t_free = sem("t_free")
        m_full = [sem(f"m_full{i}") for i in range(2)]
        m_free = [sem(f"m_free{i}") for i in range(2)]
        s_full = sem("s_full")
        s_free = sem("s_free")
        masked = sem("masked")
        pv_done = sem("pv_done")
        pv_free = sem("pv_free")
        cats_done = sem("cats_done")
        raw_done = sem("raw_done")
        qk_in = sem("qk_in")
        lines_in = sem("lines_in")
        v_held = sem("v_held")
        v_done = sem("v_done")
        mt_done = sem("mt_done")
        m_row = [sem(f"m_row{i}") for i in range(2)]

        S = [psum[:, 0:2, :], psum[:, 2:4, :]]
        M = [psum[:, 4, :], psum[:, 5, :]]
        T = psum[:, 6, :]
        PV = psum[:, 7, :]

        def heads(ap):
            return ap.rearrange("p (i h) k -> p i h k", h=H)

        def wait(eng, s, value):
            if not (isinstance(value, int) and value <= 0):
                eng.wait_ge(s, value)

        def pipeline(eng, body, counts):
            body(0, None, None)
            body(1, 0, None)
            with eng.Fori(0, NB - 2) as i:
                for c, k in counts:
                    c.enter(i, k)
                body(i + 2, i + 1, i)
                for c, k in counts:
                    c.leave(NB - 2, k)
            body(None, NB - 1, NB - 2)
            body(None, None, NB - 1)

        T_USES = 2 + 2 + 2 * NP
        T_FREES = 2 + 2 * NP
        M_WRITES = [2 + 2 + 1 + 3 * NP, 2 + 2 + 3 * NP]
        M_READS = [2 + 2 + 1 + 4 * NP, 2 + 2 + 4 * NP]
        CHAIN = IT + 5 + 10 + 2
        CONSTS = 13

        block = ctx.enter_context(nc.Block())

        @block.sync
        def _(sp):
            bias_in = bias[:, 0:3 * D]
            for dst, src in (
                (w_raw[:, 0:3 * D], dram["wqkv"]),
                (w_raw[:, 3 * D:3 * D + 4 * H], dram["w1p"]),
                (w_raw[:, 3 * D + 4 * H:], dram["w2p"]),
                (wo_raw[:], dram["wout"]),
                (bout[:], dram["bout"].partition_broadcast(P)),
                (pscale[:], dram["scale"].partition_broadcast(P)),
                (bias_in, dram["bqkv"].partition_broadcast(P)),
            ):
                if dst is bias_in:
                    sp.wait_ge(const, 1)
                sp.dma_start(dst, src).then_inc(ld, 16)

            def rows(hf, value):
                sp.wait_ge(mt_done, value)
                for hh in range(2):
                    row = qt[HP * hh + K - 1:HP * hh + K, 4 * hf:4 * hf + 4, :].bitcast(F32)
                    sp.dma_start(row.rearrange("a b (t c) -> a (b t) c", c=P),
                                 mt[4 * IT * hh:4 * IT * (hh + 1), hf, :].bitcast(F32)).then_inc(m_row[hf], 16)

            rows(0, 1)
            with sp.Fori(0, NB - 1) as i:
                rows(1, i * 2 + 2)
                rows(0, i * 2 + 3)
            rows(1, 2 * NB)
            sp.wait_ge(m_row[0], 32 * NB)
            sp.wait_ge(m_row[1], 32 * NB)

        @block.gpsimd
        def _(pool):
            nc.gpsimd.memset(bias[:], 0.0).then_inc(const, 1)
            links = 1

            def link(ins):
                nonlocal links
                links += 1
                ins.then_inc(const, 1)
                pool.wait_ge(const, links)

            nc.gpsimd.memset(qcat[:], 0.0).then_inc(const, 1)
            links += 1
            link(nc.gpsimd.memset(mx[:], 0.0))
            for hh in range(2):
                link(nc.gpsimd.memset(kt[hh][HP * (1 - hh):HP * (2 - hh)].bitcast(F32), 0.0))
            link(nc.gpsimd.memset(kcat[:], 0.0))
            link(nc.gpsimd.memset(kcat[:, :, K - 1:K], -1.0))
            link(nc.gpsimd.memset(v_sb[:], 0.0))
            link(nc.gpsimd.memset(v_sb[:, :, DH:DH + 1], 1.0))
            link(nc.gpsimd.memset(causal[:], 0.0))
            link(nc.gpsimd.affine_select(out=causal[:, BANK - P:], in_=causal[:, BANK - P:], compare_op=ALU.is_ge,
                                         fill=-3.0e38, base=0, pattern=[[-1, P]], channel_multiplier=1))
            pool.wait_ge(ld, 16 * 7)
            link(nc.gpsimd.tensor_copy(line_scale[:], pscale[:].unsqueeze(2).to_broadcast([P, H, NC])))
            link(nc.gpsimd.tensor_scalar(line_scale[:, :, 1:5:3], line_scale[:, :, 1:5:3], -1.0, None, ALU.mult))
            assert links == CONSTS
            s_n = Count()

            def exponentiated():
                pool.wait_ge(s_free, s_n.step())
                i = (s_n.local - 1) % (3 * NP)
                nc.gpsimd.tensor_tensor(gate_pool[:, i:i + 1], ident[:, 0:1], ident[:, 0:1], ALU.add)

            def keep(view, blocks):
                return nc.gpsimd.affine_select(out=view, in_=view, compare_op=ALU.is_ge, fill=0.0, base=0,
                                               pattern=[[0, blocks]] * (blocks > 1) + [[1, P]], channel_multiplier=-1)

            def body(c, b, d):
                if c is not None:
                    pool.wait_ge(xn_done, c + 1)
                    xv = x_sb[:, bass.ds(c * IT, IT), :]
                    nc.gpsimd.tensor_tensor(xv, xv, bout[:].unsqueeze(1).to_broadcast([P, IT, D]),
                                            ALU.add).then_inc(bout_added, 1)
                for p in range(NP):
                    if p == 4 and c is not None:
                        pool.wait_ge(raw_done, c + 1)
                        wait(pool, v_done, c)
                        nc.gpsimd.tensor_tensor(gate_pool[:, 3 * NP:], ident[:, 0:1], ident[:, 0:1], ALU.add)
                        nc.gpsimd.tensor_copy(v_hold[:], raw[:, :, 2 * D:3 * D]).then_inc(v_held, 1)
                    if b is None:
                        continue
                    pr = probs[:, p % PB, :]
                    for h in range(2):
                        exponentiated()
                        o = 2 * BANK * h
                        keep(pr[:, o:o + P], 1)
                        keep(pr[:, o + BANK:o + BANK + 2 * P].rearrange("p (a c) -> p a c", a=2), 2).then_inc(masked, 1)
                    exponentiated()
                    g = pr[:, 4 * BANK:].rearrange("p (a c) -> p a c", a=2)[:, :, 0:P]
                    keep(g, 2).then_inc(masked, 1)

            pipeline(pool, body, [(s_n, 3 * NP)])

        @block.scalar
        def _(act):
            t_n, s_n, g_n, pv_n = Count(), Count(), Count(), Count()

            def group(p, g, b):
                n = s_n.now()
                act.wait_ge(s_full, n + 1)
                if g == 0:
                    wait(act, pv_done, pv_n.now() - (PB - 1))
                    pv_n.step()
                src = S[(3 * p + g) % 2]
                dst = probs[:, p % PB, :]
                if g < 2:
                    out, in_ = dst[:, 2 * BANK * g:2 * BANK * (g + 1)], src.rearrange("p a c -> p (a c)")
                else:
                    out, in_ = dst[:, 4 * BANK:].rearrange("p (a c) -> p a c", a=2), src[:, :, 0:BANK // 2]
                nc.scalar.activation(out, in_, ACT.Exp).then_inc(s_free, 1)
                s_n.step()

            def take(dst, needed):
                act.wait_ge(t_full, t_n.step())
                wait(act, s_full, needed)
                nc.scalar.copy(dst, T).then_inc(t_free, 1)

            def take_keys(a, needed):
                act.wait_ge(t_full, t_n.step())
                wait(act, s_full, needed)
                nc.scalar.copy(kt[0][0:HP, a, :], T[0:HP, :])
                nc.scalar.copy(kt[1][HP:, a, :], T[HP:, :]).then_inc(t_free, 1)

            def high(dst):
                act.wait_ge(t_full, t_n.step())
                nc.scalar.copy(dst, T).then_inc(t_half, 1)

            def pv_out(g):
                act.wait_ge(pv_done, g_n.step(2))
                nc.scalar.copy(ao_t[:, g, :], PV).then_inc(pv_free, 1)

            def body(c, b, d):
                for p in range(NP):
                    if p == 3 and b is not None:
                        t_n.step()
                    if p == 7 and c is not None:
                        t_n.step()
                    if p == 1 and d is not None:
                        pv_out(3)
                    if b is not None and p in (3, 5, 7):
                        pv_out((p - 3) // 2)
                    pairs = (2 * (p - 4), 2 * (p - 4) + 1) if c is not None and p >= 4 else ()

                    def needed(a):
                        return 0 if b is None else first + 3 * a

                    if b is not None:
                        group(p, 0, b)
                    if pairs:
                        take(qt[:, pairs[0], :], needed(pairs[0]))
                    if p == 2 and d is not None:
                        high(aot_hi[:])
                    if b is not None:
                        group(p, 1, b)
                    if p == 0 and c is not None:
                        high(xt_hi[:])
                    if pairs:
                        take_keys(pairs[0], needed(pairs[0]))
                    if b is not None:
                        group(p, 2, b)
                        if p == 0:
                            first = s_n.now()
                    if p == 3 and c is not None:
                        act.wait_ge(lines_in, c + 1)
                        act.wait_ge(qk_in, c * 4 + 2)
                        for at in (0, 2 * C):
                            nc.scalar.copy(kcat[:, :, at:at + C].bitcast(F32R), kf[:]).then_inc(qk_in, 1)
                    if p == 1 and c is not None:
                        act.wait_ge(raw_done, c + 1)
                        nc.scalar.activation(heads(qf[:])[:, :, :, 0:DH],
                                             raw[:, :, 0:D].rearrange("p i (h k) -> p i h k", k=DH), ACT.Copy,
                                             scale=QSCALE).then_inc(qk_in, 1)
                        nc.scalar.copy(heads(kf[:])[:, :, :, 0:DH],
                                       raw[:, :, D:2 * D].rearrange("p i (h k) -> p i h k", k=DH)).then_inc(qk_in, 1)
                    if pairs:
                        take(qt[:, pairs[1], :], needed(pairs[1]))
                        take_keys(pairs[1], needed(pairs[1]))

            pipeline(act, body, [(t_n, T_USES), (s_n, 3 * NP), (g_n, NP), (pv_n, NP)])

        @block.vector
        def _(dve):
            chain = Count()

            def link(ins):
                ins.then_inc(link_dve, 1)
                dve.wait_ge(link_dve, chain.step())

            norm_factors(nc, link, norm)
            dve.wait_ge(ld, 16 * 7)
            link(nc.vector.tensor_copy(w_hi[:], w_raw[:]))
            nc.vector.tensor_tensor(w_lo[:], w_raw[:], w_hi[:].bitcast(F32), ALU.subtract).then_inc(w_done, 1)
            link(nc.vector.tensor_copy(wo_hi[:], wo_raw[:]))
            nc.vector.tensor_tensor(wo_lo[:], wo_raw[:], wo_hi[:].bitcast(F32), ALU.subtract).then_inc(w_done, 1)


            t_n, half_n, m_n, m_r = Count(), Count(), [Count(), Count()], [Count(), Count()]
            p1 = raw[:, :, 3 * D:3 * D + 4 * H].rearrange("p i (h k) -> p i h k", k=4)
            p2 = raw[:, :, 3 * D + 4 * H:].rearrange("p i (h k) -> p i h k", k=4)

            def filled(i):
                dve.wait_ge(m_full[i], m_n[i].step())

            def release(i, ins):
                m_r[i].step()
                return ins.then_inc(m_free[i], 1)

            def maxima_out(hf, c):
                dve.wait_ge(t_full, t_n.step())
                wait(dve, m_row[hf], c * 32)
                nc.vector.tensor_copy(mt[:, hf, :], T[0:2 * 4 * IT, 0:P]).then_inc(mt_done, 1)

            def low(dst, hi):
                t_n.step()
                dve.wait_ge(t_half, half_n.step())
                nc.vector.tensor_tensor(dst, T, hi.bitcast(F32), ALU.subtract).then_inc(t_free, 1)

            def normalise(c):
                for s in range(IT):
                    t = c * IT + s
                    last = nc.vector.tensor_scalar(
                        xn[:, P * s:P * (s + 1)], x_sb[:, bass.ds(t, 1), :].rearrange("p a d -> p (a d)"),
                        norm.mv[:, bass.ds(t, 1), 0], norm.rstd[:, bass.ds(t, 1)], ALU.subtract, ALU.mult)
                last.then_inc(xn_done, 1)

            def divide(it):
                i = it % 2
                filled(i)
                o = M[i].rearrange("p (h k) -> p h k", k=VW)
                link(nc.vector.reciprocal(rec[:, i, :], o[:, :, DH]))
                release(i, nc.vector.tensor_tensor(ao[:, it, :].rearrange("p (h k) -> p h k", k=DH), o[:, :, 0:DH],
                                                   rec[:, i, :].unsqueeze(2).to_broadcast([P, H, DH]), ALU.mult))

            def lines(c):
                for x, y, out in ((p1, p2, heads(la[:])), (p2, p1, heads(lb[:]))):
                    for i, o in ((0, 0), (1, 3), (2, 5)):
                        w = 3 - i
                        last = nc.vector.tensor_tensor(out[:, :, :, o:o + w], y[:, :, :, i + 1:4],
                                                       x[:, :, :, i:i + 1].to_broadcast([P, IT, H, w]), ALU.mult)
                link(last)
                link(nc.vector.tensor_tensor(la[:], la[:], lb[:], ALU.subtract))
                link(nc.vector.tensor_tensor(lb[:], la[:], la[:], ALU.mult))
                link(nc.vector.reduce_sum(ss[:], lb[:], AX_X))
                link(nc.vector.tensor_scalar(ss[:], ss[:], 1e-24, None, ALU.max))

            def operands(c):
                shape = [P, IT * H, NC]
                link(nc.vector.tensor_tensor(kf[:, :, DH:C], la[:], rn[:].unsqueeze(2).to_broadcast(shape), ALU.mult))
                nc.vector.tensor_tensor(heads(qf[:])[:, :, :, DH:C], heads(kf[:])[:, :, :, DH:C][:, :, :, ::-1],
                                        line_scale[:].unsqueeze(1).to_broadcast([P, IT, H, NC]),
                                        ALU.mult).then_inc(lines_in, 1)
                dve.wait_ge(lines_in, c + 1)
                dve.wait_ge(qk_in, c * 4 + 2)
                link(nc.vector.tensor_copy(qcat[:, :, 0:2 * C].bitcast(F32R).rearrange("p a (t c) -> p a t c", c=C),
                                           qf[:].unsqueeze(2).to_broadcast([P, IT * H, 2, C])))
                nc.vector.tensor_tensor(qcat[:, :, 2 * C:3 * C].bitcast(F32R), qf[:], qcat[:, :, 0:C],
                                        ALU.subtract).then_inc(cats_done, 1)
                dve.wait_ge(qk_in, c * 4 + 3)
                nc.vector.tensor_tensor(kcat[:, :, C:2 * C].bitcast(F32R), kf[:], kcat[:, :, 0:C],
                                        ALU.subtract).then_inc(cats_done, 1)

            def row_max(a, hh, it):
                w = P * (it + 1)
                o = P if it == 1 else 0
                release(hh, nc.vector.tensor_tensor_reduce(
                    out=junk[:, hh, o:o + w], in0=M[hh][:, o:o + w], in1=causal[:, BANK - w:], scale=1.0, scalar=-3.0e38,
                    op0=ALU.add, op1=ALU.max, accum_out=mx[:, a // 4, hh, a % 4, it:it + 1]))

            def bias_in_raw(c, it):
                if it == 0:
                    wait(dve, v_held, c)
                filled(it % 2)
                release(it % 2, nc.vector.tensor_tensor(raw[:, it, :], M[it % 2], bias[:], ALU.add))

            def row_maxima(a, parts=(0, 1, 2)):
                for k in parts:
                    its = ((0, 1), (2,), (3,))[k]
                    for hh in range(2):
                        filled(hh)
                        at = (a * 3 + k) * 2 + hh
                        nc.vector.memset(gate_dve[:, at:at + 1], 0.0)
                        for it in its:
                            row_max(a, hh, it)

            def copy_v(b):
                if not isinstance(b, int) or b > 0:
                    dve.wait_ge(pv_done, b * NP)
                dve.wait_ge(v_held, b + 1)
                nc.vector.tensor_copy(heads(v_sb[:])[:, :, :, 0:DH],
                                      v_hold[:].rearrange("p i (h k) -> p i h k", k=DH)).then_inc(v_done, 1)

            def body(c, b, d):
                if c is not None:
                    normalise(c)
                if b is not None:
                    row_maxima(NP - 1, (0, 1))
                if c is not None:
                    low(xt_lo[:], xt_hi[:])
                if b is not None:
                    row_maxima(NP - 1, (2,))
                if c is not None:
                    for k in range(2):
                        bias_in_raw(c, k)
                if b is not None:
                    copy_v(b)
                if c is not None:
                    for k in range(2, IT):
                        bias_in_raw(c, k)
                    for i in range(2):
                        dve.wait_ge(m_free[i], m_r[i].now())
                    nc.vector.memset(gate_dve[:, 6 * NP:6 * NP + 1], 0.0).then_inc(raw_done, 1)
                if d is not None:
                    for it in range(IT):
                        divide(it)
                if c is not None:
                    lines(c)
                if d is not None:
                    low(aot_lo[:], aot_hi[:])
                if c is not None:
                    rsqrt(nc, link, rn[:], ss[:], nw[:])
                if b is not None:
                    maxima_out(1, b)
                if c is not None:
                    if isinstance(c, int):
                        dve.wait_ge(const, CONSTS)
                    operands(c)
                if d is not None:
                    filled(0)
                    dve.wait_ge(bout_added, d + 1)
                    xv = x_sb[:, bass.ds(d * IT, IT), :]
                    release(0, nc.vector.tensor_tensor(xv, M[0].rearrange("p (a d) -> p a d", d=D), xv, ALU.add))
                    dve.wait_ge(m_free[0], m_r[0].now())
                    nc.vector.memset(gate_dve[:, 6 * NP + 1:], 0.0)
                    for s in range(IT):
                        nc.vector.bn_stats(norm.stats[:, bass.ds(d * IT + s, 1), :].rearrange("p a k -> p (a k)"),
                                           x_sb[:, bass.ds(d * IT + s, 1), :].rearrange("p a d -> p (a d)"))
                if c is not None:
                    for a in range(NP - 1):
                        if a == 5:
                            t_n.step(12)
                            maxima_out(0, c)
                            t_n.step(4)
                        row_maxima(a)

            pipeline(dve, body, [(t_n, T_USES), (half_n, 2), (m_n[0], M_WRITES[0]), (m_n[1], M_WRITES[1]),
                                 (m_r[0], M_READS[0]), (m_r[1], M_READS[1]), (chain, CHAIN)])

        @block.tensor
        def _(pe):
            t_n, t_r, mt_n, s_n, pv_n, g_n = Count(), Count(), Count(), Count(), Count(), Count()
            m_r = [Count(), Count()]

            def product(out, a_hi, a_lo, b_hi, b_lo):
                nc.tensor.matmul(out, a_hi, b_hi, start=True, stop=False)
                nc.tensor.matmul(out, a_hi, b_lo, start=False, stop=False)
                return nc.tensor.matmul(out, a_lo, b_hi, start=False, stop=True)

            def transposes(pieces, maxima=False):
                pe.wait_ge(t_free, t_r.now()) if not (isinstance(t_r.now(), int) and t_r.now() == 0) else None
                wait(pe, mt_done, mt_n.now())
                for dst, src in pieces:
                    last = nc.tensor.transpose(dst, src, ident[:])
                last.then_inc(t_full, 1)
                (mt_n if maxima else t_r).step()

            def bank(i, reads):
                wait(pe, m_free[i], m_r[i].now())
                m_r[i].step(reads)

            def maxima(hf):
                for i in range(2):
                    wait(pe, m_free[i], m_r[i].now())
                transposes([(T[0:2 * 4 * IT, 0:P], mx[:, hf, :, :, :].rearrange("p a b c -> p (a b c)"))], maxima=True)

            def pair(cat, a):
                return [(T[:, P * it:P * (it + 1)],
                         cat[:, H * it + 2 * a:H * it + 2 * a + 2, :].rearrange("p a c -> p (a c)")) for it in range(IT)]

            def logits(p, g):
                n = s_n.step()
                wait(pe, s_free, n - 2)
                s = S[(3 * p + g) % 2]

                def one(hh, jt, out):
                    return nc.tensor.matmul(out, kt[hh][:, p, P * jt:P * (jt + 1)], qt[:, p, P * jt:], start=True, stop=True)

                if g < 2:
                    one(g, 0, s[:, 0, :])
                    one(g, 3, s[:, 1, 0:P])
                    one(g, 1, s[:, 1, P:]).then_inc(s_full, 1)
                else:
                    one(0, 2, s[:, 0, 0:2 * P])
                    one(1, 2, s[:, 1, 0:2 * P]).then_inc(s_full, 1)

            def values(p, k):
                hh, jt = k % 2, k // 2
                h = 2 * p + hh
                out = PV[VW * (h % 4):VW * (h % 4 + 1), P * jt:]
                at = (2 * BANK * hh, 2 * BANK * hh + BANK + P, 4 * BANK + 2 * P * hh, 2 * BANK * hh + BANK)[jt]
                if k == 0:
                    pe.wait_ge(masked, pv_n.now() * 3 + 3)
                    if p % 2 == 0:
                        wait(pe, pv_free, g_n.now())
                        g_n.step()
                last = nc.tensor.matmul(out, v_sb[:, H * jt + h, :], probs[:, p % PB, at:at + BANK - P * jt],
                                        start=jt == 0, stop=jt == 3)
                if k == 7:
                    last.then_inc(pv_done, 1)
                    pv_n.step()

            def row_logits(a, part, hh):
                bank(hh, 2 if part == 0 else 1)
                for it in (0, 1) if part == 0 else (part + 1,):
                    w = P * (it + 1)
                    o = P if it == 1 else 0
                    last = nc.tensor.matmul(M[hh][:, o:o + w], qt[:, a, P * it:P * (it + 1)], kt[hh][:, a, 0:w],
                                            start=True, stop=True)
                last.then_inc(m_full[hh], 1)

            def project(c, it):
                bank(it % 2, 1)
                t = slice(P * it, P * (it + 1))
                product(M[it % 2], xt_hi[:, t], xt_lo[:, t], w_hi[:], w_lo[:]).then_inc(m_full[it % 2], 1)

            def divide_in(it):
                bank(it % 2, 1)
                for g in range(H // 4):
                    last = nc.tensor.transpose(M[it % 2][:, P * g:P * (g + 1)], ao_t[:, g, P * it:P * (it + 1)], ident[:])
                last.then_inc(m_full[it % 2], 1)

            def out_project():
                pe.wait_ge(w_done, 2)
                pe.wait_ge(t_free, t_r.now())
                bank(0, 1)
                for it in range(IT):
                    t = slice(P * it, P * (it + 1))
                    last = product(M[0][:, P * it:P * (it + 1)], aot_hi[:, t], aot_lo[:, t], wo_hi[:], wo_lo[:])
                last.then_inc(m_full[0], 1)

            def body(c, b, d):
                def lg(p, g):
                    if b is not None:
                        if g == 0 and p in (0, 4):
                            pe.wait_ge(m_row[p // 4], b * 32 + 32)
                        logits(p, g)

                def pv(p, *ks):
                    if (b if p else d) is not None:
                        for k in ks:
                            if p == 1 and k == 0:
                                pe.wait_ge(v_done, b + 1)
                            values((p - 1) % NP, k)

                lg(0, 0)
                if b is not None:
                    pe.wait_ge(t_free, t_r.now())
                pv(0, 0, 1)
                lg(0, 1)
                for i in range(6):
                    if b is not None:
                        row_logits(NP - 1, i // 2, i % 2)
                    if i == 1:
                        lg(0, 2)
                        if c is not None:
                            pe.wait_ge(xn_done, c + 1)
                            transposes([(T[:, P * s:P * (s + 1)], xn[:, P * s:P * (s + 1)]) for s in range(IT)])
                    if i < 5:
                        pv(0, i + 2)
                if c is not None:
                    pe.wait_ge(w_done, 1)
                    pe.wait_ge(t_free, t_r.now())
                    project(c, 0)
                    project(c, 1)
                pv(0, 7)
                lg(1, 0)
                if c is not None:
                    project(c, 2)
                lg(1, 1)
                pv(1, 0)
                if c is not None:
                    project(c, 3)
                pv(1, 1)
                lg(1, 2)
                pv(1, 2)
                if d is not None:
                    pe.wait_ge(pv_free, d * 4 + 4)
                    divide_in(0)
                pv(1, 3)
                if d is not None:
                    divide_in(1)
                pv(1, 4)
                if d is not None:
                    divide_in(2)
                pv(1, 5)
                if d is not None:
                    divide_in(3)
                pv(1, 6, 7)
                lg(2, 0)
                pv(2, 0, 1)
                if d is not None:
                    for i in range(2):
                        pe.wait_ge(m_free[i], m_r[i].now())
                    transposes([(T[:, P * it:P * (it + 1)], ao[:, it, :]) for it in range(IT)])
                lg(2, 1)
                pv(2, 2, 3)
                lg(2, 2)
                pv(2, 4, 5, 6)
                pv(2, 7)
                lg(3, 0)
                if b is not None:
                    maxima(1)
                lg(3, 1)
                pv(3, 0, 1)
                pv(3, 2, 3)
                lg(3, 2)
                pv(3, 4, 5, 6)
                if d is not None:
                    out_project()
                pv(3, 7)
                for p in range(4, NP):
                    a = 2 * (p - 4)
                    if c is not None:
                        if p == 4:
                            if isinstance(c, int):
                                pe.wait_ge(const, CONSTS)
                            pe.wait_ge(cats_done, c * 2 + 2)
                            pe.wait_ge(qk_in, c * 4 + 4)

                    def turn(cat, n):
                        if c is not None:
                            transposes(pair(cat, n))

                    def rl(n, part, hh):
                        if c is not None and n >= 0:
                            row_logits(n, part, hh)

                    lg(p, 0)
                    if p == 7 and c is not None:
                        pv(p, 0)
                        maxima(0)
                    turn(qcat, a)
                    rl(a - 1, 0, 0)
                    if p < 7 or c is None:
                        pv(p, 0)
                    rl(a - 1, 0, 1)
                    lg(p, 1)
                    turn(kcat, a)
                    pv(p, 1)
                    rl(a - 1, 1, 0)
                    lg(p, 2)
                    rl(a - 1, 1, 1)
                    pv(p, 2, 3)
                    rl(a - 1, 2, 0)
                    rl(a - 1, 2, 1)
                    turn(qcat, a + 1)
                    pv(p, 4)
                    rl(a, 0, 0)
                    rl(a, 0, 1)
                    turn(kcat, a + 1)
                    pv(p, 5)
                    rl(a, 1, 0)
                    rl(a, 1, 1)
                    pv(p, 6)
                    rl(a, 2, 0)
                    pv(p, 7)
                    rl(a, 2, 1)

            pipeline(pe, body, [(t_r, T_FREES), (mt_n, 2), (s_n, 3 * NP), (pv_n, NP), (g_n, NP // 2),
                                (m_r[0], M_READS[0]), (m_r[1], M_READS[1])])


def ffn_phase(nc, tag, psum, x_sb, ident, norm, dram, x_in, y_out):
    NT = x_sb.shape[1]
    D = x_sb.shape[2]
    TOK = NT * P
    NE, _, F = dram["w_gate"].shape
    FC = F // P
    TT = TOK // BANK
    SUB = BANK // P
    NR = 2 * NE
    WCOLS = 3 * F
    CHUNK = WCOLS // TT
    GU_CHUNKS = -(-2 * F // CHUNK)
    HALF = TOK // 2
    assert D == P and FC == 4 and NE % 2 == 0 and WCOLS % TT == 0 and NT * NR == BANK

    with ExitStack() as ctx:
        def sb(name, shape, dt=F32):
            return ctx.enter_context(nc.sbuf_tensor(f"{name}_{tag}", shape, dt))

        def sem(name):
            return ctx.enter_context(nc.semaphore(f"{name}_{tag}"))

        xt_hi = sb("xt_hi", [P, TOK], F32R)
        xt_lo = sb("xt_lo", [P, TOK], F32R)
        f_acc = sb("f_acc", [P, TOK])
        f_sum = sb("f_sum", [P, 2, BANK])
        tiny = sb("tiny", [P, 1])
        gate_dve = sb("gate_dve", [P, 2])
        w_raw = sb("w_raw", [P, 2, WCOLS])
        w_hi = sb("w_hi", [P, 2, WCOLS], F32R)
        w_lo = sb("w_lo", [P, 2, WCOLS], F32R)
        wr_raw = sb("wr_raw", [P, P])
        wr_hi = sb("wr_hi", [P, P], F32R)
        wr_lo = sb("wr_lo", [P, P], F32R)
        xn = sb("xn", [P, 2, BANK])
        logit_t = sb("logit_t", [NR, TOK])
        probs = sb("probs", [P, NT, 2, NE])
        red = sb("red", [P, NT * 2])
        cw = sb("cw", [P, 2, NE, NT // 2])
        cws = sb("cws", [P, NT])
        cw_rows = sb("cw_rows", [P, 2, P])
        cwb = sb("cwb", [P, 2, TOK])
        s_buf = sb("s_buf", [P, 2, BANK])
        h_buf = sb("h_buf", [P, 2, BANK])
        h_hi = sb("h_hi", [P, FC, BANK], F32R)
        h_lo = sb("h_lo", [P, FC, BANK], F32R)
        o_tmp = sb("o_tmp", [P, BANK])

        x_ld = [sem(f"x_ld{i}") for i in range(TT)]
        w_ld = [sem(f"w_ld{i}") for i in range(2)]
        cwb_ld = [sem(f"cwb_ld{i}") for i in range(2)]
        wr_ld = sem("wr_ld")
        wr_zero = sem("wr_zero")
        f_zero = sem("f_zero")
        dve_link = sem("dve_link")
        tiny_set = sem("tiny_set")
        xn_done = sem("xn_done")
        xt_tr = sem("xt_tr")
        xt_hi_done = sem("xt_hi_done")
        xt_lo_done = sem("xt_lo_done")
        w0_hi = sem("w0_hi")
        w0_done = sem("w0_done")
        wr_done = sem("wr_done")
        logit_mm = sem("logit_mm")
        logit_cp = sem("logit_cp")
        logit_tr = sem("logit_tr")
        shifted = sem("shifted")
        exp_done = sem("exp_done")
        cw_done = sem("cw_done")
        cw_tr = sem("cw_tr")
        cw_cp = sem("cw_cp")
        cw_st = sem("cw_st")
        gu_done = sem("gu_done")
        silu_done = sem("silu_done")
        h_done = sem("h_done")
        hi_done = sem("hi_done")
        lo_done = sem("lo_done")
        down_done = sem("down_done")
        o_read = sem("o_read")
        o_added = sem("o_added")
        w_chunk = sem("w_chunk")
        w_chunk_hi = sem("w_chunk_hi")
        f_tr = sem("f_tr")
        x_new = sem("x_new")
        y_st = sem("y_st")

        G = [psum[:, 0, :], psum[:, 1, :]]
        U = [psum[:, 2, :], psum[:, 3, :]]
        def O(t):
            return psum[:, bass.ds(4 + t % 2, 1), :].rearrange("p a c -> p (a c)")

        XT = [psum[:, 6, :], psum[:, 7, :]]
        LT = [psum[:, 4, :], psum[:, 5, :]]
        LG = psum[:, 6, :]
        CT = psum[:, 7, 0:2 * P]
        FT = [psum[:, 6, :], psum[:, 7, :]]

        def wait(eng, s, value):
            if not (isinstance(value, int) and value <= 0):
                eng.wait_ge(s, value)

        def over_tiles(eng, tile):
            def expert(n0, e, par, lead):
                for t in range(lead):
                    tile(n0 + t, e, t, t % 2, par)
                with eng.Fori(0, (TT - lead) // 2) as i:
                    for k in range(2):
                        t = i * 2 + (lead + k)
                        tile(i * 2 + n0 + (lead + k) if isinstance(n0, int) else n0 + t, e, t, (lead + k) % 2, par)
                tile(n0 + TT - 1, e, TT - 1, (TT - 1) % 2, par)

            expert(0, 0, 0, 3)
            with eng.Fori(0, NE // 2 - 1) as m:
                for d in (1, 2):
                    expert(m * (2 * TT) + TT * d, 2 * m + d, d % 2, 1)
            expert(TT * (NE - 1), NE - 1, 1, 3)

        block = ctx.enter_context(nc.Block())

        @block.sync
        def _(sp):
            if x_in is not None:
                x_view = x_in.rearrange("(t p) d -> p t d", p=P)
                for j in range(TT):
                    sp.dma_start(x_sb[:, SUB * j:SUB * (j + 1), :],
                                 x_view[:, SUB * j:SUB * (j + 1), :]).then_inc(x_ld[j], 16)

            def load_expert(e, par):
                sp.dma_start(w_raw[:, par, 0:F],
                             dram["w_gate"][bass.ds(e, 1)].rearrange("a k f -> k (a f)")).then_inc(w_ld[par], 16)
                sp.dma_start(w_raw[:, par, F:2 * F],
                             dram["w_up"][bass.ds(e, 1)].rearrange("a k f -> k (a f)")).then_inc(w_ld[par], 16)
                sp.dma_start(w_raw[:, par, 2 * F:].rearrange("p (c h) -> p c h", c=FC),
                             dram["w_down"][bass.ds(e, 1)].rearrange("a (c p) h -> p (a c) h",
                                                                     p=P)).then_inc(w_ld[par], 16)

            def load_cw(e, par):
                for c in range(2):
                    sp.dma_start(cwb[:, par, HALF * c:HALF * (c + 1)],
                                 dram["cw_rows_" + tag][c, bass.ds(e, 1), :].partition_broadcast(P)
                                 ).then_inc(cwb_ld[par], 16)

            sp.wait_ge(wr_zero, 1)
            sp.dma_start(wr_raw[:, 0:NE], dram["w_router"]).then_inc(wr_ld, 16)
            sp.dma_start(wr_raw[:, NE:NR], dram["w_gating"]).then_inc(wr_ld, 16)
            load_expert(0, 0)
            load_expert(1, 1)
            sp.wait_ge(cw_cp, 1)
            for c in range(2):
                sp.dma_start(dram["cw_rows_" + tag][c].rearrange("e (t p) -> (e t) p", p=P),
                             cw_rows[:, c, :]).then_inc(cw_st, 16)
            sp.wait_ge(cw_st, 32)
            load_cw(0, 0)
            load_cw(1, 1)
            sp.wait_ge(w0_done, 1)
            load_expert(2, 0)
            sp.wait_ge(o_read, TT + 1)
            load_cw(2, 0)
            with sp.Fori(0, (NE - 4) // 2) as m:
                for d in (3, 4):
                    e = 2 * m + d
                    sp.wait_ge(w_chunk, m * (2 * TT) + TT * (d - 2))
                    load_expert(e, d % 2)
                    sp.wait_ge(o_read, m * (2 * TT) + (TT * (d - 1) + 1))
                    load_cw(e, d % 2)
            e = NE - 1
            sp.wait_ge(w_chunk, TT * (e - 2))
            load_expert(e, 1)
            sp.wait_ge(o_read, TT * (e - 1) + 1)
            load_cw(e, 1)
            if y_out is not None:
                y_view = y_out.rearrange("(t p) d -> p t d", p=P)
                for j in range(TT):
                    sp.wait_ge(x_new, j + 1)
                    sp.dma_start(y_view[:, SUB * j:SUB * (j + 1), :],
                                 x_sb[:, SUB * j:SUB * (j + 1), :]).then_inc(y_st, 16)
                sp.wait_ge(y_st, 16 * TT)

        @block.gpsimd
        def _(pool):
            nc.gpsimd.memset(wr_raw[:], 0.0).then_inc(wr_zero, 1)
            nc.gpsimd.memset(f_acc[:], 0.0).then_inc(f_zero, 1)

            def low_part(q, f):
                pool.wait_ge(hi_done, q + 1)
                nc.gpsimd.tensor_tensor(h_lo[:, f, :], h_buf[:, f % 2, :], h_hi[:, f, :].bitcast(F32),
                                        ALU.subtract).then_inc(lo_done, 1)

            with pool.Fori(0, TT * NE) as n:
                for f in range(FC):
                    low_part(n * FC + f, f)

        @block.scalar
        def _(act):
            act.wait_ge(tiny_set, 1)
            nc.scalar.activation(tiny[:], tiny[:], ACT.Exp)
            act.wait_ge(w_ld[0], 48)
            nc.scalar.copy(w_hi[:, 0, :], w_raw[:, 0, :]).then_inc(w0_hi, 1)

            def high_xt(j, b):
                act.wait_ge(xt_tr, j + 1)
                nc.scalar.copy(xt_hi[:, bass.ts(j, BANK)], XT[b]).then_inc(xt_hi_done, 1)

            def copy_logits(j, b):
                act.wait_ge(logit_mm, j + 1)
                nc.scalar.copy(logit_t[:, bass.ts(j, BANK)], LT[b][0:NR, :]).then_inc(logit_cp, 1)

            high_xt(0, 0)
            high_xt(1, 1)
            with act.Fori(0, TT // 2 - 1) as i:
                for b in range(2):
                    high_xt(i * 2 + (b + 2), b)
                    copy_logits(i * 2 + b, b)
            copy_logits(TT - 2, 0)
            copy_logits(TT - 1, 1)
            act.wait_ge(shifted, 1)
            nc.scalar.activation(probs[:, :, 0, :], probs[:, :, 0, :], ACT.Exp).then_inc(exp_done, 1)
            nc.scalar.activation(probs[:, :, 1, :], probs[:, :, 1, :], ACT.Exp, scale=10.0).then_inc(exp_done, 1)

            def silu(q, f):
                act.wait_ge(gu_done, q + 1)
                wait(act, h_done, q - 1)
                nc.scalar.activation(s_buf[:, f % 2, :], G[f % 2], ACT.Silu).then_inc(silu_done, 1)

            def high_part(q, f):
                act.wait_ge(h_done, q + 1)
                wait(act, down_done, q - (FC - 1))
                nc.scalar.copy(h_hi[:, f, :], h_buf[:, f % 2, :]).then_inc(hi_done, 1)

            def tile(n):
                for f in range(FC):
                    silu(n * FC + f, f)
                    high_part(n * FC + f, f)

            tile(0)
            with act.Fori(1, TT * NE) as n:
                tile(n)

        @block.vector
        def _(dve):
            links = [0]

            def link(ins):
                links[0] += 1
                ins.then_inc(dve_link, 1)
                dve.wait_ge(dve_link, links[0])

            nc.vector.engine_nop().then_inc(o_read, 1)
            nc.vector.engine_nop().then_inc(o_added, 1)
            nc.vector.memset(tiny[:], 0.0).then_inc(tiny_set, 1)
            if x_in is not None:
                for t in range(NT):
                    if t % SUB == 0:
                        dve.wait_ge(x_ld[t // SUB], 16)
                    last = nc.vector.bn_stats(norm.stats[:, t, :], x_sb[:, t, :])
                link(last)
            norm_factors(nc, link, norm)
            dve.wait_ge(wr_ld, 32)
            link(nc.vector.tensor_copy(wr_hi[:], wr_raw[:]))
            nc.vector.tensor_tensor(wr_lo[:], wr_raw[:], wr_hi[:].bitcast(F32), ALU.subtract).then_inc(wr_done, 1)

            def normalise(j, b):
                wait(dve, xt_tr, j - 1)
                for s in range(SUB):
                    t = j * SUB + s
                    last = nc.vector.tensor_scalar(
                        xn[:, b, P * s:P * (s + 1)], x_sb[:, bass.ds(t, 1), :].rearrange("p a d -> p (a d)"),
                        norm.mv[:, bass.ds(t, 1), 0], norm.rstd[:, bass.ds(t, 1)], ALU.subtract, ALU.mult)
                last.then_inc(xn_done, 1)

            def low_xt(j, b):
                dve.wait_ge(xt_hi_done, j + 1)
                nc.vector.tensor_tensor(xt_lo[:, bass.ts(j, BANK)], XT[b], xt_hi[:, bass.ts(j, BANK)].bitcast(F32),
                                        ALU.subtract).then_inc(xt_lo_done, 1)

            normalise(0, 0)
            normalise(1, 1)
            with dve.Fori(0, TT // 2 - 1) as i:
                for b in range(2):
                    low_xt(i * 2 + b, b)
                    normalise(i * 2 + (b + 2), b)
            low_xt(TT - 2, 0)
            low_xt(TT - 1, 1)
            dve.wait_ge(w0_hi, 1)
            nc.vector.tensor_tensor(w_lo[:, 0, :], w_raw[:, 0, :], w_hi[:, 0, :].bitcast(F32),
                                    ALU.subtract).then_inc(w0_done, 1)

            dve.wait_ge(logit_tr, 1)
            lg = LG.rearrange("p (a e) -> p a e", e=NE)
            pr = probs[:].rearrange("p t s e -> p (t s) e")
            wide = [P, NT * 2, NE]
            link(nc.vector.reduce_max(red[:], lg, AX_X))
            nc.vector.tensor_tensor(pr, lg, red[:].unsqueeze(2).to_broadcast(wide), ALU.subtract).then_inc(shifted, 1)
            dve.wait_ge(exp_done, 2)
            link(nc.vector.reduce_sum(red[:], pr, AX_X))
            link(nc.vector.reciprocal(red[:], red[:]))
            link(nc.vector.tensor_tensor(pr, pr, red[:].unsqueeze(2).to_broadcast(wide), ALU.mult))
            link(nc.vector.tensor_tensor(probs[:, :, 0, :], probs[:, :, 0, :], probs[:, :, 1, :], ALU.mult))
            link(nc.vector.reduce_sum(cws[:], probs[:, :, 0, :], AX_X))
            link(nc.vector.tensor_scalar(cws[:], cws[:], 1e-9, None, ALU.add))
            link(nc.vector.reciprocal(cws[:], cws[:]))
            for c in range(2):
                last = nc.vector.tensor_tensor(
                    cw[:, c, :, :].rearrange("p e t -> p t e"), probs[:, NT // 2 * c:NT // 2 * (c + 1), 0, :],
                    cws[:, NT // 2 * c:NT // 2 * (c + 1)].unsqueeze(2).to_broadcast([P, NT // 2, NE]), ALU.mult)
            last.then_inc(cw_done, 1)

            def multiply(q, f):
                dve.wait_ge(silu_done, q + 1)
                wait(dve, lo_done, q - 1)
                nc.vector.tensor_tensor(h_buf[:, f % 2, :], U[f % 2], s_buf[:, f % 2, :],
                                        ALU.mult).then_inc(h_done, 1)

            def weigh(n, t, par, e):
                dve.wait_ge(cwb_ld[par], 32 * (e // 2 + 1) if isinstance(e, int) else e * 16 + (32 - 16 * par))
                dve.wait_ge(down_done, (n + 1) * FC)
                dve.wait_ge(o_added, n + 1)
                nc.vector.tensor_tensor(o_tmp[:], O(t), cwb[:, par, bass.ts(t, BANK)], ALU.mult).then_inc(o_read, 1)

            def add(n, t, last_expert):
                dve.wait_ge(o_read, n + 2)
                if last_expert:
                    wait(dve, f_tr, t - 1)
                    b = last_expert[0]
                    nc.vector.tensor_tensor(f_sum[:, b, :], f_acc[:, bass.ts(t, BANK)], o_tmp[:],
                                            ALU.add).then_inc(o_added, 1)
                else:
                    nc.vector.tensor_tensor(f_acc[:, bass.ts(t, BANK)], f_acc[:, bass.ts(t, BANK)], o_tmp[:],
                                            ALU.add).then_inc(o_added, 1)

            def residual(j, b):
                dve.wait_ge(f_tr, j + 1)
                xv = x_sb[:, bass.ds(j * SUB, SUB), :]
                nc.vector.scalar_tensor_tensor(xv, FT[b].rearrange("p (a d) -> p a d", d=D), 0.5, xv,
                                               ALU.mult, ALU.add).then_inc(x_new, 1)
                if y_out is None:
                    dve.wait_ge(x_new, j + 1)
                    nc.vector.memset(gate_dve[:, b:b + 1], 0.0)
                    for s in range(SUB):
                        t = j * SUB + s
                        nc.vector.bn_stats(norm.stats[:, bass.ds(t, 1), :].rearrange("p a k -> p (a k)"),
                                           x_sb[:, bass.ds(t, 1), :].rearrange("p a d -> p (a d)"))

            def tile(n, e, t, b, par):
                final = isinstance(e, int) and e == NE - 1
                new = isinstance(t, int) and t == 0
                first = isinstance(n, int) and n < 3
                pe, pt, ppar = (e - 1, TT - 1, 1 - par) if new else (e, t - 1, par)
                to_sum = (1 - b,) if final and not new else ()
                multiply(n * FC, 0)
                if first and n == 2:
                    weigh(0, 0, 0, 0)
                multiply(n * FC + 1, 1)
                if first and n == 2:
                    add(0, 0, ())
                if not first or n == 2:
                    weigh(n - 1, pt, ppar, pe)
                multiply(n * FC + 2, 2)
                if not first or n == 2:
                    add(n - 1, pt, to_sum)
                if first and n == 0:
                    dve.wait_ge(cw_tr, 1)
                    nc.vector.tensor_copy(cw_rows[:].rearrange("p c q -> p (c q)"), CT).then_inc(cw_cp, 1)
                cols = bass.ts(t, CHUNK)
                if not final:
                    dve.wait_ge(w_ld[1 - par],
                                48 * ((e + 1) // 2 + 1) if isinstance(e, int) else e * 24 + (72 - 24 * (1 - par)))
                    nc.vector.tensor_copy(w_hi[:, 1 - par, cols], w_raw[:, 1 - par, cols]).then_inc(w_chunk_hi, 1)
                multiply(n * FC + 3, 3)
                if not final:
                    dve.wait_ge(w_chunk_hi, n + 1)
                    nc.vector.tensor_tensor(w_lo[:, 1 - par, cols], w_raw[:, 1 - par, cols],
                                            w_hi[:, 1 - par, cols].bitcast(F32), ALU.subtract).then_inc(w_chunk, 1)
                elif not isinstance(t, int) or t >= 2:
                    residual(t - 2, b)

            dve.wait_ge(f_zero, 1)
            over_tiles(dve, tile)
            last_n = TT * NE - 1
            weigh(last_n, TT - 1, 1, NE - 1)
            add(last_n, TT - 1, ((TT - 1) % 2,))
            residual(TT - 2, 0)
            residual(TT - 1, 1)

        @block.tensor
        def _(pe):
            def product(out, a_hi, a_lo, b_hi, b_lo, start, stop):
                nc.tensor.matmul(out, a_hi, b_hi, start=start, stop=False)
                nc.tensor.matmul(out, a_hi, b_lo, start=False, stop=False)
                return nc.tensor.matmul(out, a_lo, b_hi, start=False, stop=stop)

            def turn(j, b):
                pe.wait_ge(xn_done, j + 1)
                wait(pe, xt_lo_done, j - 1)
                for s in range(SUB):
                    last = nc.tensor.transpose(XT[b][:, P * s:P * (s + 1)], xn[:, b, P * s:P * (s + 1)], ident[:])
                last.then_inc(xt_tr, 1)

            def router(j, b):
                pe.wait_ge(xt_lo_done, j + 1)
                wait(pe, logit_cp, j - 1)
                cols = bass.ts(j, BANK)
                product(LT[b], wr_hi[:], wr_lo[:], xt_hi[:, cols], xt_lo[:, cols], True, True).then_inc(logit_mm, 1)

            turn(0, 0)
            turn(1, 1)
            pe.wait_ge(wr_done, 1)
            for j in range(2):
                turn(j + 2, j)
                router(j, j)
            with pe.Fori(1, TT // 2 - 1) as i:
                for b in range(2):
                    turn(i * 2 + (b + 2), b)
                    router(i * 2 + b, b)
            router(TT - 2, 0)
            router(TT - 1, 1)
            pe.wait_ge(logit_cp, TT)
            for t in range(NT):
                last = nc.tensor.transpose(LG[:, NR * t:NR * (t + 1)], logit_t[:, P * t:P * (t + 1)], ident[0:NR, 0:NR])
            last.then_inc(logit_tr, 1)
            pe.wait_ge(w0_done, 1)

            def gate_up(q, f, t, par):
                wait(pe, h_done, q - 1)
                cols = bass.ts(t, BANK)
                for dst, at in ((G[f % 2], f * P), (U[f % 2], F + f * P)):
                    w = slice(at, at + P)
                    last = product(dst, w_hi[:, par, w], w_lo[:, par, w], xt_hi[:, cols], xt_lo[:, cols], True, True)
                last.then_inc(gu_done, 1)

            def down(q, f, par, n, t):
                pe.wait_ge(lo_done, q + 1)
                if f == 0:
                    wait(pe, o_read, n)
                w = slice(2 * F + f * P, 2 * F + (f + 1) * P)
                product(O(t), w_hi[:, par, w], w_lo[:, par, w], h_hi[:, f, :], h_lo[:, f, :],
                        f == 0, f == FC - 1).then_inc(down_done, 1)

            def turn_back(j, b):
                pe.wait_ge(o_added, j + (TT * (NE - 1) + 2))
                wait(pe, x_new, j - 1)
                for s in range(SUB):
                    last = nc.tensor.transpose(FT[b][:, P * s:P * (s + 1)], f_sum[:, b, P * s:P * (s + 1)], ident[:])
                last.then_inc(f_tr, 1)

            def tile(n, e, t, b, par):
                new = isinstance(t, int) and t == 0
                first = isinstance(n, int) and n == 0
                if new and not first:
                    pe.wait_ge(w_chunk, n - (TT - GU_CHUNKS))
                for f in range(FC):
                    q = n * FC + f
                    gate_up(q, f, t, par)
                    if f >= 2:
                        if new and not first and f == 2:
                            pe.wait_ge(w_chunk, n)
                        down(q - 2, f - 2, par, n, t)
                    elif not first:
                        down(q - 2, f + 2, 1 - par if new else par, n - 1, TT - 1 if new else t - 1)
                    if f == 0 and isinstance(e, int) and e == NE - 1 and not (isinstance(t, int) and t < 2):
                        turn_back(t - 2, b)
                    if first and f == 2:
                        pe.wait_ge(cw_done, 1)
                        for c in range(2):
                            last = nc.tensor.transpose(CT[:, P * c:P * (c + 1)], cw[:, c, :, :].rearrange("p e t -> p (e t)"), ident[:])
                        last.then_inc(cw_tr, 1)

            over_tiles(pe, tile)
            last_q = TT * NE * FC
            down(last_q - 2, 2, 1, TT * NE - 1, TT - 1)
            down(last_q - 1, 3, 1, TT * NE - 1, TT - 1)
            turn_back(TT - 2, 0)
            turn_back(TT - 1, 1)


def macaron_block(nc, x, wqkv, bqkv, w1p, w2p, scale, wout, bout, w_router, w_gating, w_gate, w_up, w_down, out):
    D = x.shape[2]
    tokens = x.shape[0] * x.shape[1]
    NE = w_gate.shape[0]
    assert x.shape[1] == BANK, "a block of 512 columns is a sequence of the attention"
    x_rows, out_rows = (a.rearrange("b t d -> (b t) d") for a in (x, out))
    ffn = dict(w_router=w_router, w_gating=w_gating, w_gate=w_gate, w_up=w_up, w_down=w_down)
    for tag in ("f1", "f2"):
        ffn["cw_rows_" + tag] = nc.dram_tensor("cw_dram_" + tag, (2, NE, tokens // 2), F32, kind="Internal").ap()
    with ExitStack() as ctx:
        psum = ctx.enter_context(nc.psum_tensor("psum", [P, 8, BANK], F32))
        x_sb = ctx.enter_context(nc.sbuf_tensor("x_sb", [P, tokens // P, D], F32))
        ident = ctx.enter_context(nc.sbuf_tensor("ident", [P, P], F32))
        norm = Norm(*(ctx.enter_context(nc.sbuf_tensor("norm_" + name, [P, tokens // P, *rest], F32)) for name, *rest in
                      (("stats", 6), ("mv", 2), ("var",), ("rstd",), ("scratch",))))
        ident_zero = ctx.enter_context(nc.semaphore("ident_zero"))
        with nc.Block() as block:
            @block.gpsimd
            def _(pool):
                nc.gpsimd.memset(ident[:], 0.0).then_inc(ident_zero, 1)
                pool.wait_ge(ident_zero, 1)
                nc.gpsimd.affine_select(out=ident[:], in_=ident[:], compare_op=ALU.not_equal, fill=1.0, base=0,
                                        pattern=[[-1, P]], channel_multiplier=1).then_inc(ident_zero, 1)
                pool.wait_ge(ident_zero, 2)
        ffn_phase(nc, "f1", psum, x_sb, ident, norm, ffn, x_rows, None)
        attention_phase(nc, psum, x_sb, ident, norm, dict(wqkv=wqkv, bqkv=bqkv, w1p=w1p, w2p=w2p, scale=scale,
                                                          wout=wout, bout=bout))
        ffn_phase(nc, "f2", psum, x_sb, ident, norm, ffn, None, out_rows)


_INS = ["L0_attn_x", "L0_attn_Wqkv", "L0_attn_bqkv", "L0_attn_W1p", "L0_attn_W2p", "L0_attn_plucker_scale",
        "L0_attn_Wout", "L0_attn_bout", "L0_ffn_w_router", "L0_ffn_w_gating", "L0_ffn_w_gate", "L0_ffn_w_up",
        "L0_ffn_w_down"]


def kernel(**inputs):
    import numpy as _np
    import concourse.bacc as _bacc
    from concourse import mybir as _mybir
    from concourse.bass_utils import run_bass_kernel_spmd as _run

    nc = _bacc.Bacc("TRN2", target_bir_lowering=False, num_devices=1)
    arrays, args = {}, []
    for name in _INS:
        a = _np.ascontiguousarray(inputs[name])
        arrays[f"in_{name}_dram"] = a
        args.append(nc.dram_tensor(f"in_{name}_dram", a.shape, _mybir.dt.from_np(a.dtype), kind="ExternalInput").ap())
    out = nc.dram_tensor("out_0_dram", inputs["L0_attn_x"].shape, _mybir.dt.float32, kind="ExternalOutput").ap()
    macaron_block(nc, *args, out)
    r = _run(nc, [arrays], core_ids=[0])
    return r.results[0]["out_0_dram"]
```
